# Optimizing a Trainium2 kernel written in Bass

```python
import numpy as np
import jax
import jax.numpy as jnp

def _softmax(x, axis=-1):
    return jax.nn.softmax(x, axis=axis)

def _gelu(x):
    return jax.nn.gelu(x, approximate=True)

def _silu(x):
    return jax.nn.silu(x)

def _sigmoid(x):
    return jax.nn.sigmoid(x)

def _layernorm(x, axis=-1, eps=1e-05):
    m = jnp.mean(x, axis=axis, keepdims=True)
    v = jnp.var(x, axis=axis, keepdims=True)
    return (x - m) / jnp.sqrt(v + eps)

def _scatter_add(tgt, idx, src, axis=0):
    return tgt.at[idx].add(src)

def _segment_sum(src, seg, n):
    return jax.ops.segment_sum(src, seg, n)
kernel_name = 'mk_seq_postln_d1_jaxref_r4_5e6651'

def setup_inputs(seed: int=0):
    np.random.seed(seed)
    _w = jnp.asarray

    def _L0_attn_setup():
        import math
        import jax, jax.numpy as jnp
        import numpy as np
        B, S, DIM, HEADS = (1, 512, 256, 16)
        HEAD_DIM = DIM // HEADS
        key = jax.random.key(seed)
        ks = jax.random.split(key, 6)
        scale = DIM ** (-0.5)
        x = jax.random.normal(ks[0], (B, S, DIM), jnp.float32)
        wq = jax.random.normal(ks[1], (DIM, DIM), jnp.float32) * scale
        wk = jax.random.normal(ks[2], (DIM, DIM), jnp.float32) * scale
        wv = jax.random.normal(ks[3], (DIM, DIM), jnp.float32) * scale
        wo = jax.random.normal(ks[4], (DIM, DIM), jnp.float32) * scale
        pope_bias = -jax.random.uniform(ks[5], (HEADS, HEAD_DIM), jnp.float32) * 3.0
        return {'x': x, 'wq': wq, 'wk': wk, 'wv': wv, 'wo': wo, 'pope_bias': pope_bias}
    _L0_attn_in = _L0_attn_setup()

    def _L0_ffn_setup():
        import math
        import jax, jax.numpy as jnp
        import numpy as np
        D_MODEL = 256
        D_HIDDEN = 1024
        N_EXPERTS = 8
        TOP_K = 2
        CAPACITY_FACTOR = 1.25
        key = jax.random.key(seed)
        ks = jax.random.split(key, 8)
        s = 0.02
        x = jax.random.normal(ks[0], (4, 512, D_MODEL), dtype=jnp.float32)
        router_w = jax.random.normal(ks[1], (D_MODEL, N_EXPERTS), dtype=jnp.float32) * s
        router_b = jnp.zeros((N_EXPERTS,), dtype=jnp.float32)
        w1 = jax.random.normal(ks[2], (N_EXPERTS, D_MODEL, D_HIDDEN), dtype=jnp.float32) * s
        b1 = jnp.zeros((N_EXPERTS, D_HIDDEN), dtype=jnp.float32)
        w2 = jax.random.normal(ks[3], (N_EXPERTS, D_HIDDEN, D_MODEL), dtype=jnp.float32) * s
        b2 = jnp.zeros((N_EXPERTS, D_MODEL), dtype=jnp.float32)
        return {'x': x, 'router_w': router_w, 'router_b': router_b, 'w1': w1, 'b1': b1, 'w2': w2, 'b2': b2}
    _L0_ffn_in = _L0_ffn_setup()
    _d = {'L0_attn_x': _L0_attn_in['x'], 'L0_attn_wq': _L0_attn_in['wq'], 'L0_attn_wk': _L0_attn_in['wk'], 'L0_attn_wv': _L0_attn_in['wv'], 'L0_attn_wo': _L0_attn_in['wo'], 'L0_attn_pope_bias': _L0_attn_in['pope_bias'], 'L0_ffn_router_w': _L0_ffn_in['router_w'], 'L0_ffn_router_b': _L0_ffn_in['router_b'], 'L0_ffn_w1': _L0_ffn_in['w1'], 'L0_ffn_b1': _L0_ffn_in['b1'], 'L0_ffn_w2': _L0_ffn_in['w2'], 'L0_ffn_b2': _L0_ffn_in['b2']}
    _x0 = _d['L0_attn_x']
    _d['L0_attn_x'] = jax.random.normal(jax.random.fold_in(jax.random.key(seed), 1), (4, 1024, 256), dtype=_x0.dtype)
    del _x0
    return _d

def reference(L0_attn_x, L0_attn_wq, L0_attn_wk, L0_attn_wv, L0_attn_wo, L0_attn_pope_bias, L0_ffn_router_w, L0_ffn_router_b, L0_ffn_w1, L0_ffn_b1, L0_ffn_w2, L0_ffn_b2):

    def _L0_attn_ref(x, wq, wk, wv, wo, pope_bias):
        import math
        import jax, jax.numpy as jnp
        import numpy as np
        B, S, DIM, HEADS = (1, 512, 256, 16)
        HEAD_DIM = DIM // HEADS
        B_, S_, C = x.shape
        H = HEADS
        D = C // H
        q = jnp.einsum('bsc,oc->bso', x, wq).reshape(B_, S_, H, D).transpose(0, 2, 1, 3)
        k = jnp.einsum('bsc,oc->bso', x, wk).reshape(B_, S_, H, D).transpose(0, 2, 1, 3)
        v = jnp.einsum('bsc,oc->bso', x, wv).reshape(B_, S_, H, D).transpose(0, 2, 1, 3)
        inv_freqs = 10000.0 ** (-(jnp.arange(D, dtype=jnp.float32) / D))
        pos = jnp.arange(S_, dtype=jnp.float32)
        freqs = pos[:, None] * inv_freqs[None, :]
        bias = jnp.clip(pope_bias, -2.0 * math.pi, 0.0)
        freqs_with_bias = freqs[None, :, :] + bias[:, None, :]
        q_mag = jax.nn.softplus(q)
        k_mag = jax.nn.softplus(k)
        qp = freqs[None, None, :, :]
        kp = freqs_with_bias[None, :, :, :]
        q_embed = jnp.stack([q_mag * jnp.cos(qp), q_mag * jnp.sin(qp)], axis=-1).reshape(B_, H, S_, 2 * D)
        k_embed = jnp.stack([k_mag * jnp.cos(kp), k_mag * jnp.sin(kp)], axis=-1).reshape(B_, H, S_, 2 * D)
        scores = jnp.einsum('bhsd,bhtd->bhst', q_embed, k_embed) / D ** 0.5
        attn = jax.nn.softmax(scores, axis=-1)
        out = jnp.einsum('bhst,bhtd->bhsd', attn, v)
        out = out.transpose(0, 2, 1, 3).reshape(B_, S_, C)
        return jnp.einsum('bsc,oc->bso', out, wo)

    def _L0_ffn_ref(x, router_w, router_b, w1, b1, w2, b2):
        import math
        import jax, jax.numpy as jnp
        import numpy as np
        D_MODEL = 256
        D_HIDDEN = 1024
        N_EXPERTS = 8
        TOP_K = 2
        CAPACITY_FACTOR = 1.25
        B, T, D = x.shape
        N = B * T
        E = N_EXPERTS
        capacity = max(1, math.ceil(N / E * CAPACITY_FACTOR))
        x_flat = x.reshape(N, D)
        logits = x_flat.astype(jnp.float32) @ router_w + router_b
        gates = jax.nn.softmax(logits, axis=-1)
        _, topk_idx = jax.lax.top_k(gates, TOP_K)
        expert_mask = jax.nn.one_hot(topk_idx, E, dtype=jnp.int32).sum(1)
        pos = jnp.cumsum(expert_mask, axis=0) - 1
        expert_mask = expert_mask * (pos < capacity)
        valid = expert_mask > 0
        pos_c = jnp.where(valid, pos, capacity)
        e_idx = jnp.broadcast_to(jnp.arange(E), (N, E))
        dispatched = x_flat[:, None, :] * valid[:, :, None].astype(x.dtype)
        buf = jnp.zeros((E, capacity + 1, D), x.dtype).at[e_idx.ravel(), pos_c.ravel()].add(dispatched.reshape(N * E, D))
        buf = buf[:, :capacity]
        h = jax.nn.gelu(jnp.einsum('ecd,edh->ech', buf, w1) + b1[:, None, :], approximate=False)
        out = jnp.einsum('ech,ehd->ecd', h, w2) + b2[:, None, :]
        pos_g = jnp.minimum(pos_c, capacity - 1)
        gathered = out[e_idx, pos_g]
        weights = (gates * valid).astype(x.dtype)
        y = jnp.einsum('ned,ne->nd', gathered, weights)
        return y.reshape(B, T, D)
    x = L0_attn_x
    x = _layernorm(x + _L0_attn_ref(x, L0_attn_wq, L0_attn_wk, L0_attn_wv, L0_attn_wo, L0_attn_pope_bias), axis=-1)
    x = _layernorm(x + _L0_ffn_ref(x, L0_ffn_router_w, L0_ffn_router_b, L0_ffn_w1, L0_ffn_b1, L0_ffn_w2, L0_ffn_b2), axis=-1)
    return x

_drawn_inputs = setup_inputs


def setup_inputs(seed=0):
    import zlib

    import numpy as np

    out = dict(_drawn_inputs(seed))
    spreads = {'L0_ffn_router_b': (0.0, 0.473), 'L0_ffn_b1': (0.0, 0.8), 'L0_ffn_b2': (0.0, 0.4)}
    factors = {}
    for name, (base, spread) in spreads.items():
        noise = np.random.default_rng([zlib.crc32(name.encode()), seed]).standard_normal(out[name].shape)
        drawn = base * np.exp(spread * noise) if base else spread * noise
        out[name] = jnp.asarray(drawn.astype(out[name].dtype))
    for name, factor in factors.items():
        out[name] = (out[name] * factor).astype(out[name].dtype)
    return out
```

```python
from contextlib import ExitStack

import concourse.bass as bass
from concourse import mybir

F32 = mybir.dt.float32
F32R = mybir.dt.float32r
BF16 = mybir.dt.bfloat16
I32 = mybir.dt.int32
ALU = mybir.AluOpType
ACT = mybir.ActivationFunctionType
AX = mybir.AxisListType

P = 128
BATCH, SEQ, DIM, HEADS = 4, 1024, 256, 16
HD = DIM // HEADS
EXPERTS, HIDDEN = 8, 1024
TOKENS = BATCH * SEQ
CAP = -(-TOKENS * 5 // (EXPERTS * 4))
SLOTS = EXPERTS * CAP
EPS = 1e-5
PI = 3.1415927410125732

KC = DIM // P
TB = SEQ // P
GH = 4
GROUPS = HEADS // GH
HALF = SEQ // 2
STEPS = 2 * TB
NG = BATCH * GROUPS
NSTEP = NG * STEPS
ROWS = 3 * 2 * HD
BOUND = 60.0
ST = CAP // P
HK = HIDDEN // P
CH = CAP // 2
OOB = 2 * SLOTS


def misc_schedule():
    at = {}

    def put(s, job):
        at.setdefault(s, []).append(job)

    for i in range(4):
        put(-13 + 3 * i, ("qk", 0, i))
        put(-12 + 3 * i, ("v", 0, i))
        put(-10 + 3 * i, ("norms", 0, i))
    put(-1, ("count", 0))
    for grp in range(0, NG - 2, 2):
        c, s0 = grp // 2 + 1, STEPS * grp
        for i in range(4):
            put(s0 + (2, 5, 10, 13)[i], ("qk", c, i))
            put(s0 + (5, 9, 14, 17)[i], ("norms", c, i))
        put(s0 + 18, ("count", c))
        if grp % GROUPS == 2:
            for i in range(4):
                put(s0 + STEPS + (4, 7, 12, 15)[i], ("v", grp // GROUPS + 1, i))
    for b in range(BATCH):
        s0, t = STEPS * GROUPS * (b + 1), TAIL[b == BATCH - 1]
        for i in range(4):
            put(s0 + t["project"][i], ("project", b, i))
            put(s0 + t["turn"][i], ("turn", b, i))
            put(s0 + t["router"][i], ("router", b, i))
        put(s0 + t["place"], ("place", b))
    return at


TAIL = {
    False: dict(project=(8, 9, 11, 12), rstd=14, norm=15, turn=(19, 21, 23, 26), router=(20, 22, 25, 28),
                exp=29, top=30, place=31),
    True: dict(project=(4, 5, 6, 7), rstd=8, norm=9, turn=(10, 12, 14, 16), router=(11, 13, 15, 17),
               exp=18, top=19, place=20),
}


def build(nc, x_d, xT_d, wq_d, wk_d, wv_d, wo_d, bias_d, wr_d, br_d, w1_d, b1_d, w2_d, b2_d,
          trig_d, ident_d, tri_d, blocks_d, rev_d, base_d, out):
    jobs = misc_schedule()
    first, last = min(jobs), NSTEP + TAIL[True]["place"] + 1
    number, n = {}, 0
    for s in range(first, last + 1):
        for job in jobs.get(s, ()):
            number[job] = n
            n += 1

    split_d = nc.dram_tensor("split_scratch", (2, BATCH, 2, HEADS, 2 * HD, SEQ), F32).ap()
    disp_d = nc.dram_tensor("dispatched", (SLOTS, DIM), F32).ap()
    x1_d = nc.dram_tensor("x1_scratch", (TOKENS, DIM), F32).ap()
    eo_d = nc.dram_tensor("expert_out", (SLOTS, DIM), F32).ap()

    with ExitStack() as both:
        sb2 = lambda name, shape, dt=F32: both.enter_context(nc.sbuf_tensor(name, shape, dt))
        ident = sb2("ident", [P, P])
        gather_idx = sb2("gather_idx", [P, BATCH * TB, 2], I32)
        gate_w = sb2("gate_w", [P, BATCH * TB, 2])
        attention(nc, jobs, number, first, last, x_d, xT_d, wq_d, wk_d, wv_d, wo_d, bias_d, wr_d,
                  br_d, trig_d, ident_d, tri_d, blocks_d, rev_d, base_d, split_d, disp_d,
                  x1_d, ident, gather_idx, gate_w)
        experts(nc, w1_d, b1_d, w2_d, b2_d, disp_d, x1_d, eo_d, ident, gather_idx, gate_w, out)


def attention(nc, jobs, number, first, last, x_d, xT_d, wq_d, wk_d, wv_d, wo_d, bias_d, wr_d, br_d,
              trig_d, ident_d, tri_d, blocks_d, rev_d, base_d, split_d, disp_d, x1_d,
              ident, gather_idx, gate_w):
    with ExitStack() as ctx:
        sb = lambda name, shape, dt=F32: ctx.enter_context(nc.sbuf_tensor(name, shape, dt))
        sem = lambda name: ctx.enter_context(nc.semaphore(name))

        qtrig = sb("qtrig", [P, 2, SEQ])
        ktrig = sb("ktrig", [P, KC, 2, SEQ])
        wqkv = sb("wqkv", [P, 3, KC, DIM])
        woT = sb("woT", [P, KC, DIM])
        wr = sb("wr", [P, KC, EXPERTS])
        br = sb("br", [P, EXPERTS])
        tri_f = sb("tri_f", [P, P])
        tri = sb("tri", [P, P], BF16)
        ones = sb("ones", [P, P], BF16)
        blocks_f = sb("blocks_f", [P, P])
        blocks = sb("blocks", [P, P], BF16)
        square = sb("square", [P, HALF], BF16)
        ones_col = sb("ones_col", [P, 1])
        rev = sb("rev", [P, TB, EXPERTS])
        slot_base = sb("slot_base", [P, TB, EXPERTS])
        zeros = sb("zeros", [P, DIM])
        ang = sb("ang", [P, 6, KC])
        xT = sb("xT", [P, KC, SEQ])
        raw = sb("raw", [P, HALF])
        soft = sb("soft", [P, HALF])
        emb = sb("emb", [P, 2, HALF])
        split = [sb(f"split{i}", [P, 2, 2, HALF], F32R) for i in range(2)]
        tops = sb("tops", [P, 4])
        top2 = sb("top2", [P, 3])
        over = sb("over", [P, 1])
        flags = sb("flags", [1, NG // 2], I32)
        qst = [sb(f"qst{i}", [ROWS + 1, GH, SEQ], F32R) for i in range(2)]
        kst = [sb(f"kst{i}", [ROWS + 1, GH, SEQ], F32R) for i in range(2)]
        val = [sb(f"val{i}", [P, TB, HEADS, HD + 1]) for i in range(2)]
        NPB, NSB = 4, 3
        prob = [sb(f"prob{i}", [P, 2 * HALF]) for i in range(NPB)]
        oraw = sb("oraw", [P, HALF])
        oden = sb("oden", [P, HALF])
        onorm = sb("onorm", [P, HALF])
        aT = sb("aT", [P, KC, SEQ])
        res = sb("res", [P, TB, DIM])
        stats = sb("stats", [P, TB, 6])
        mv = sb("mv", [P, TB, 2])
        lnt = sb("lnt", [P, 5, TB])
        x1T = sb("x1T", [P, 2, KC, P])
        rt = sb("rt", [P, 12, TB, EXPERTS])
        rs = sb("rs", [P, 16, TB])
        mask = sb("mask", [P, TB, EXPERTS], BF16)
        before = sb("before", [P, EXPERTS], BF16)
        scatter_idx = sb("scatter_idx", [P, 2, TB], I32)
        gmax = sb("gmax", [P, 2 * GH * TB])
        gneg = sb("gneg", [P, GH * TB])
        grow = sb("grow", [GH * TB, P], F32R)

        spsum = [ctx.enter_context(nc.psum_tensor(f"spsum{i}", [P, 2, HALF], F32)) for i in range(NSB)]
        opsum = ctx.enter_context(nc.psum_tensor("opsum", [P, HALF], F32))
        misc = ctx.enter_context(nc.psum_tensor("misc", [P, HALF], F32))

        s_wqk, s_trig, s_wv = sem("s_wqk"), sem("s_trig"), sem("s_wv")
        s_setup, s_sums = sem("s_setup"), sem("s_sums")
        s_raw, s_hi = sem("s_raw"), sem("s_hi")
        s_const, s_xT, s_res, s_zero = sem("s_const"), sem("s_xT"), sem("s_res"), sem("s_zero")
        s_init = sem("s_init")
        s_chain = sem("s_chain")
        s_actchain = sem("s_actchain")
        s_angle, s_sin = sem("s_angle"), sem("s_sin")
        s_full, s_free = sem("s_misc_full"), sem("s_misc_free")
        s_abs, s_soft = sem("s_abs"), sem("s_soft")
        s_split = sem("s_split")
        s_store = [sem(f"s_store{i}") for i in range(4)]
        s_square, s_over, s_flag = sem("s_square"), sem("s_over"), sem("s_flag")
        s_fill = [sem(f"s_fill{i}") for i in range(2)]
        s_score, s_exp, s_pv = sem("s_score"), sem("s_exp"), sem("s_pv")
        s_ofree, s_norm, s_aT = sem("s_ofree"), sem("s_onorm"), sem("s_aT")
        s_var, s_rstd, s_x1 = sem("s_var"), sem("s_rstd"), sem("s_x1")
        s_logit, s_gexp, s_mask, s_idx = sem("s_logit"), sem("s_gexp"), sem("s_mask"), sem("s_idx")
        s_scat, s_x1d = sem("s_scat"), sem("s_x1d")
        g_full, g_free, g_row = sem("s_gen_full"), sem("s_gen_free"), sem("s_gen_row")
        GEN = 2 * GH * TB

        NCONST = 8
        block = ctx.enter_context(nc.Block())

        def jobs_at(s):
            return jobs.get(s, ())

        def tail_at(s, what):
            for b in range(BATCH):
                if s == STEPS * GROUPS * (b + 1) + TAIL[b == BATCH - 1][what]:
                    return b
            return None

        @block.sync
        def _(sp):
            sp.dma_start(wqkv[:, 0], wq_d).then_inc(s_wqk, 16)
            sp.dma_start(xT[:], xT_d[0]).then_inc(s_xT, 16)
            sp.dma_start(wqkv[:, 1], wk_d).then_inc(s_wqk, 16)
            sp.dma_start(ang[:, 0, :], bias_d).then_inc(s_trig, 16)
            sp.dma_start(qtrig[:], trig_d).then_inc(s_trig, 16)
            sp.dma_start(wqkv[:, 2], wv_d).then_inc(s_wv, 16)
            sp.dma_start(woT[:], wo_d).then_inc(s_const, 16)
            sp.dma_start(wr[:], wr_d).then_inc(s_const, 16)
            sp.dma_start(br[:], br_d.to_broadcast((P, EXPERTS))).then_inc(s_const, 16)
            sp.dma_start(ident[:], ident_d).then_inc(s_const, 16)
            sp.dma_start(tri_f[:], tri_d).then_inc(s_const, 16)
            sp.dma_start(blocks_f[:], blocks_d).then_inc(s_const, 16)
            sp.dma_start(rev[:].rearrange("p t e -> p (t e)"), rev_d).then_inc(s_const, 16)
            sp.dma_start(slot_base[:].rearrange("p t e -> p (t e)"), base_d).then_inc(s_const, 16)
            sp.dma_start(res[:], x_d[0]).then_inc(s_res, 16)

            def fill(grp):
                b, h0, par = grp // GROUPS, GH * (grp % GROUPS), grp % 2
                for i in range(4):
                    sp.wait_ge(s_store[i], 32 * (grp // 2 + 1))
                if grp >= 2:
                    sp.wait_ge(s_score, 2 * STEPS * (grp - 1))
                for qk, stack, terms in ((0, qst, (0, 0, 1)), (1, kst, (0, 1, 0))):
                    for r, part in enumerate(terms):
                        sp.dma_start(stack[par][2 * HD * r:2 * HD * (r + 1)].bitcast(F32),
                                     split_d[qk, b, part, h0:h0 + GH].rearrange("h r n -> r h n")
                                     ).then_inc(s_fill[par], 16)
                sp.dma_start(qst[par][ROWS:ROWS + 1].bitcast(F32),
                             zeros[0:GH * SEQ // DIM, :]).then_inc(s_fill[par], 16)
                sp.wait_ge(s_flag, grp // 2 + 1)
                flag = sp.value_load(flags[0:1, grp // 2:grp // 2 + 1], min_val=0, max_val=P)
                with sp.If(flag > 0):
                    sp.wait_ge(g_free, (GEN + 2) * (grp + 1))
                    sp.wait_ge(s_fill[par], 112 * (grp // 2 + 1))
                    sp.dma_start(qst[par][ROWS:ROWS + 1].bitcast(F32),
                                 grow[:].bitcast(F32)).then_inc(g_row, 16)
                with sp.Else():
                    sp.sem_inc(g_row, 16)

            def gather_heads(blk):
                b, g, qh = blk // (2 * GROUPS), blk // 2 % GROUPS, blk % 2
                sp.wait_ge(s_norm, blk + 1)
                if b and blk % (2 * GROUPS) == 0:
                    sp.wait_ge(s_full, number["project", b - 1, 3] + 1)
                for j in range(GH):
                    r = (g % 2) * GH * HD + HD * j
                    sp.dma_start(aT[r:r + HD, g // 2, HALF * qh:HALF * (qh + 1)],
                                 onorm[32 * j:32 * j + HD, :]).then_inc(s_aT, 16)

            sp.wait_ge(s_init, 1)
            fill(0)
            fill(1)
            for grp in range(NG):
                b = grp // GROUPS
                if grp:
                    gather_heads(2 * grp - 1)
                if 1 <= grp < NG - 1:
                    fill(grp + 1)
                if grp % GROUPS == 1 and b < BATCH - 1:
                    sp.wait_ge(s_full, number["qk", 2 * b + 1, 3] + 1)
                    sp.dma_start(xT[:], xT_d[b + 1]).then_inc(s_xT, 16)
                if grp % GROUPS == 3 and b:
                    sp.wait_ge(s_scat, 16 * 2 * TB * b)
                    sp.wait_ge(s_x1d, 16 * b)
                    sp.dma_start(res[:], x_d[b]).then_inc(s_res, 16)
                gather_heads(2 * grp)
            gather_heads(2 * NG - 1)

        @block.gpsimd
        def _(pool):
            def clear_slots():
                pool.wait_ge(s_init, 1)
                pool.dma_start(disp_d.rearrange("(p t) d -> p t d", p=P),
                               zeros[:].unsqueeze(1).to_broadcast((P, SLOTS // P, DIM))
                               ).then_inc(s_zero, 16)

            def store_split(c, i):
                b, ct, qk, half = c // KC, c % KC, i % 2, i // 2
                u = 4 * c + i
                pool.wait_ge(s_raw, u + 1)
                if u:
                    pool.wait_ge(s_full, number["norms", (u - 1) // 4, (u - 1) % 4] + 1)
                pool.tensor_tensor(square[:], raw[:], raw[:], ALU.mult).then_inc(s_square, 1)
                pool.wait_ge(s_hi, u + 1)
                pool.tensor_tensor(split[u % 2][:, 1], emb[:], split[u % 2][:, 0].bitcast(F32),
                                   ALU.subtract).then_inc(s_split, 1)
                pool.wait_ge(s_split, u + 1)
                for part in range(2):
                    pool.dma_start(
                        split_d[qk, b, part, 8 * ct:8 * ct + 8, :, HALF * half:HALF * (half + 1)]
                        .rearrange("h (d t) n -> (h d) t n", t=2),
                        split[u % 2][:, part].bitcast(F32)).then_inc(s_store[i], 16)

            def scatter(b):
                pool.wait_ge(s_x1, b + 1)
                pool.dma_start(x1_d[b * SEQ:(b + 1) * SEQ].rearrange("(t p) d -> p t d", p=P),
                               res[:]).then_inc(s_x1d, 16)
                pool.wait_ge(s_idx, b + 1)
                pool.wait_ge(s_zero, 16)
                for t in range(TB):
                    for k in range(2):
                        pool.indirect_dma_start(
                            disp_d, bass.IndirectOffsetOnAxis(ap=scatter_idx[:, k, t:t + 1], axis=0),
                            res[:, t, :], None, bounds_check=SLOTS - 1,
                            oob_is_err=False).then_inc(s_scat, 16)

            def normalise(blk):
                pool.wait_ge(s_sums, blk + 1)
                if blk:
                    pool.wait_ge(s_aT, 16 * GH * blk)
                pool.tensor_tensor(onorm[:], oraw[:], oden[:], ALU.mult).then_inc(s_norm, 1)

            for s in range(first, last + 1):
                for job in jobs_at(s - 2):
                    if job[0] == "qk":
                        store_split(*job[1:])
                if s == 0:
                    clear_slots()
                if TB <= s - 2 <= NSTEP and (s - 2) % TB == 0:
                    normalise((s - 2) // TB - 1)
                for job in jobs_at(s):
                    if job[0] == "place":
                        scatter(job[1])
            pool.wait_ge(s_scat, 16 * 2 * TB * BATCH)
            pool.wait_ge(s_x1d, 16 * BATCH)

        @block.scalar
        def _(act):
            done = [0]

            def chained(ins):
                done[0] += 1
                ins.then_inc(s_actchain, 1)
                act.wait_ge(s_actchain, done[0])

            act.wait_ge(s_angle, 1)
            act.activation(ang[:, 3:5, :], ang[:, 1:3, :], ACT.Sin).then_inc(s_sin, 1)
            act.preload_act_table_set("natural_log_exp_and_others")

            def softplus(u):
                act.wait_ge(s_abs, u + 1)
                chained(act.activation(soft[:], soft[:], ACT.Exp))
                act.activation(soft[:], soft[:], ACT.Ln, bias=1.0).then_inc(s_soft, 1)

            def rstd_guess(b):
                act.wait_ge(s_var, b + 1)
                chained(act.activation(lnt[:, 1, :], lnt[:, 0, :], ACT.Ln))
                act.activation(lnt[:, 2, :], lnt[:, 1, :], ACT.Exp, scale=-0.5).then_inc(s_rstd, 1)

            def gates_exp(b):
                act.wait_ge(s_logit, b + 1)
                act.activation(rt[:, 1], rt[:, 1], ACT.Exp).then_inc(s_gexp, 1)

            for s in range(first, last + 1):
                if 0 <= s < NSTEP:
                    for u in (2 * s, 2 * s + 1):
                        act.wait_ge(s_score, u + 1)
                        if u >= NPB:
                            act.wait_ge(s_pv, (u - NPB) // 2 + 1)
                        act.activation(prob[u % NPB][:], spsum[u % NSB][:].rearrange("p a n -> p (a n)"),
                                       ACT.Exp, scale=HD ** -0.5).then_inc(s_exp, 1)
                for job in jobs_at(s - 1):
                    if job[0] == "qk":
                        softplus(4 * job[1] + job[2])
                if (b := tail_at(s, "rstd")) is not None:
                    rstd_guess(b)
                if (b := tail_at(s, "exp")) is not None:
                    gates_exp(b)

        @block.tensor
        def _(pe):
            def begin(job):
                if number[job]:
                    pe.wait_ge(s_free, number[job])

            def run(job):
                kind, c, i = (*job, 0)[:3]
                begin(job)
                if kind == "qk":
                    ct, qk, half = c % KC, i % 2, i // 2
                    pe.wait_ge(s_wqk, 32)
                    pe.wait_ge(s_xT, 16 * (c // KC + 1))
                    for k in range(KC):
                        ins = pe.matmul(misc[:], wqkv[:, qk, k, P * ct:P * (ct + 1)],
                                        xT[:, k, HALF * half:HALF * (half + 1)],
                                        start=k == 0, stop=k == KC - 1)
                elif kind == "v":
                    pe.wait_ge(s_wv, 16)
                    pe.wait_ge(s_xT, 16 * (c + 1))
                    for t in range(2):
                        for k in range(KC):
                            tok = P * (2 * i + t)
                            ins = pe.matmul(misc[:, DIM * t:DIM * (t + 1)], xT[:, k, tok:tok + P],
                                            wqkv[:, 2, k, :], start=k == 0, stop=k == KC - 1)
                elif kind == "norms":
                    pe.wait_ge(s_setup, 1)
                    pe.wait_ge(s_square, 4 * c + i + 1)
                    ins = pe.matmul(misc[:], blocks[:], square[:], start=True, stop=True)
                elif kind == "count":
                    pe.wait_ge(s_over, c + 1)
                    ins = pe.matmul(misc[0:1, 0:1], over[:], ones_col[:], start=True, stop=True)
                elif kind == "project":
                    pe.wait_ge(s_aT, 16 * GH * 2 * GROUPS * (c + 1))
                    pe.wait_ge(s_const, 16 * NCONST)
                    for t in range(2):
                        for k in range(KC):
                            tok = P * (2 * i + t)
                            ins = pe.matmul(misc[:, DIM * t:DIM * (t + 1)], aT[:, k, tok:tok + P],
                                            woT[:, k, :], start=k == 0, stop=k == KC - 1)
                elif kind == "turn":
                    pe.wait_ge(s_x1, c + 1)
                    for t in range(2):
                        for k in range(KC):
                            ins = pe.transpose(misc[:, P * (KC * t + k):P * (KC * t + k + 1)],
                                               res[:, 2 * i + t, P * k:P * (k + 1)], ident[:])
                elif kind == "router":
                    for t in range(2):
                        for k in range(KC):
                            ins = pe.matmul(misc[:, EXPERTS * t:EXPERTS * (t + 1)], x1T[:, t, k, :],
                                            wr[:, k, :], start=k == 0, stop=k == KC - 1)
                elif kind == "place":
                    pe.wait_ge(s_mask, c + 1)
                    pos = misc[:, 0:TB * EXPERTS].rearrange("p (t e) -> p t e", e=EXPERTS)
                    pe.matmul(pos, tri[:], mask[:], start=True, stop=False)
                    for t in range(TB - 1):
                        pe.matmul(pos[:, t + 1:TB, :], ones[:],
                                  mask[:, t:t + 1, :].to_broadcast((P, TB - 1 - t, EXPERTS)),
                                  start=False, stop=False)
                    ins = pe.matmul(pos, ones[:], before[:].unsqueeze(1).to_broadcast((P, TB, EXPERTS)),
                                    start=False, stop=True)
                ins.then_inc(s_full, 1)

            def general_maxima(grp, jobs_before):
                par = grp % 2
                pe.wait_ge(s_flag, grp // 2 + 1)
                flag = pe.value_load(flags[0:1, grp // 2:grp // 2 + 1], min_val=0, max_val=P)
                with pe.If(flag > 0):
                    pe.wait_ge(s_free, jobs_before)
                    base = (GEN + 2) * grp
                    for j in range(GH):
                        for t in range(TB):
                            for half in range(2):
                                m = (j * TB + t) * 2 + half
                                if base + m:
                                    pe.wait_ge(g_free, base + m)
                                pe.matmul(misc[:], qst[par][0:ROWS, j, P * t:P * (t + 1)],
                                          kst[par][0:ROWS, j, HALF * half:HALF * (half + 1)],
                                          start=True, stop=True).then_inc(g_full, 1)
                    pe.wait_ge(g_free, base + GEN + 1)
                    pe.transpose(misc[0:GH * TB, 0:P], gneg[:], ident[:]).then_inc(g_full, 1)
                    pe.wait_ge(g_row, 16 * (grp + 1))
                with pe.Else():
                    pe.sem_inc(g_full, GEN + 1)

            def scores(s):
                grp, qh, kt = s // STEPS, s // TB % 2, s % TB
                par = grp % 2
                for pair in range(2):
                    u = 2 * s + pair
                    if u >= NSB:
                        pe.wait_ge(s_exp, u - NSB + 1)
                    for e in range(2):
                        j = 2 * pair + e
                        ins = pe.matmul(spsum[u % NSB][:, e, :], kst[par][:, j, P * kt:P * (kt + 1)],
                                        qst[par][:, j, HALF * qh:HALF * (qh + 1)], start=True, stop=True)
                    ins.then_inc(s_score, 1)

            def values(s):
                grp, kt = s // STEPS, s % TB
                b, h0 = grp // GROUPS, GH * (grp % GROUPS)
                pe.wait_ge(s_exp, 2 * s + 2)
                if kt == 0 and s >= TB:
                    pe.wait_ge(s_ofree, s // TB)
                for j in range(GH):
                    ins = pe.matmul(opsum[32 * j:32 * j + HD + 1, :], val[b % 2][:, kt, h0 + j, :],
                                    prob[(2 * s + j // 2) % NPB][:, HALF * (j % 2):HALF * (j % 2 + 1)],
                                    start=kt == 0, stop=kt == TB - 1)
                ins.then_inc(s_pv, 1)

            ran = 0
            for s in range(first, last + 1):
                if 0 <= s < NSTEP:
                    if s % STEPS == 0:
                        grp = s // STEPS
                        pe.wait_ge(s_fill[grp % 2], 112 * (grp // 2 + 1))
                        general_maxima(grp, ran)
                    scores(s)
                for job in jobs_at(s):
                    run(job)
                    ran += 1
                if 0 < s <= NSTEP:
                    if (s - 1) % (STEPS * GROUPS) == 0:
                        b = (s - 1) // (STEPS * GROUPS)
                        pe.wait_ge(s_free, number["v", b, 3] + 1)
                    values(s - 1)

        @block.vector
        def _(dve):
            links = [0]

            def link(ins):
                links[0] += 1
                ins.then_inc(s_chain, 1)
                dve.wait_ge(s_chain, links[0])

            counts = {}

            def tell(ins, s):
                counts[s.name] = counts.get(s.name, 0) + 1
                ins.then_inc(s, 1)
                dve.wait_ge(s, counts[s.name])

            link(dve.memset(ones_col[:], 1.0))
            link(dve.memset(opsum[:], 0.0))
            for i in range(2):
                link(dve.memset(kst[i][ROWS:ROWS + 1].bitcast(F32), 1.0))
            tell(dve.memset(zeros[:], 0.0), s_init)
            dve.wait_ge(s_trig, 32)
            link(dve.tensor_scalar(ang[:, 1, :], ang[:, 0, :], -2 * PI, 0.0, ALU.max, ALU.min))
            link(dve.tensor_scalar(ang[:, 1, :], ang[:, 1, :], PI, None, ALU.add))
            link(dve.scalar_tensor_tensor(ang[:, 2, :], ang[:, 1, :], -1.0, ang[:, 1, :], ALU.mult, ALU.min))
            tell(dve.tensor_scalar(ang[:, 2, :], ang[:, 2, :], PI / 2, None, ALU.add), s_angle)
            dve.wait_ge(s_sin, 1)
            link(dve.tensor_scalar(ang[:, 5, :], ang[:, 3, :], -1.0, None, ALU.mult))
            link(dve.tensor_scalar(ang[:, 4, :], ang[:, 4, :], -1.0, None, ALU.mult))

            def key_angles(ct):
                cosb, sinb, nsinb = ang[:, 4, ct:ct + 1], ang[:, 5, ct:ct + 1], ang[:, 3, ct:ct + 1]
                link(dve.tensor_scalar(ktrig[:, ct, 0, :], qtrig[:, 1, :], nsinb, None, ALU.mult))
                link(dve.scalar_tensor_tensor(ktrig[:, ct, 0, :], qtrig[:, 0, :], cosb,
                                              ktrig[:, ct, 0, :], ALU.mult, ALU.add))
                link(dve.tensor_scalar(ktrig[:, ct, 1, :], qtrig[:, 0, :], sinb, None, ALU.mult))
                link(dve.scalar_tensor_tensor(ktrig[:, ct, 1, :], qtrig[:, 1, :], cosb,
                                              ktrig[:, ct, 1, :], ALU.mult, ALU.add))

            def set_up():
                for i in range(2):
                    link(dve.memset(val[i][:, :, :, HD:HD + 1], 1.0))
                link(dve.memset(ones[:], 1.0))
                link(dve.memset(before[:], 0.0))
                dve.wait_ge(s_const, 16 * NCONST)
                link(dve.tensor_copy(tri[:], tri_f[:]))
                tell(dve.tensor_copy(blocks[:], blocks_f[:]), s_setup)

            def split_unit(c, i):
                ct, qk, half = c % KC, i % 2, i // 2
                u = 4 * c + i
                dve.wait_ge(s_soft, u + 1)
                tell(dve.scalar_tensor_tensor(raw[:], raw[:], 0.0, soft[:], ALU.max, ALU.add), s_raw)
                table = qtrig[:] if qk == 0 else ktrig[:, ct]
                if u:
                    dve.wait_ge(s_split, u)
                link(dve.tensor_tensor(emb[:], raw[:].unsqueeze(1).to_broadcast((P, 2, HALF)),
                                       table[:, :, HALF * half:HALF * (half + 1)], ALU.mult))
                if u >= 2:
                    v = u - 2
                    dve.wait_ge(s_store[v % 4], 32 * (v // 4 + 1))
                tell(dve.tensor_copy(split[u % 2][:, 0], emb[:]), s_hi)

            def read_out(job):
                kind, c, i = (*job, 0)[:3]
                dve.wait_ge(s_full, number[job] + 1)
                if kind == "qk":
                    if u := 4 * c + i:
                        dve.wait_ge(s_square, u)
                    tell(dve.tensor_copy(raw[:], misc[:]), s_free)
                    tell(dve.scalar_tensor_tensor(soft[:], raw[:], -1.0, raw[:], ALU.mult, ALU.min), s_abs)
                elif kind == "v":
                    tell(dve.tensor_copy(val[c % 2][:, 2 * i:2 * i + 2, :, 0:HD],
                                         misc[:].rearrange("p (t h d) -> p t h d", t=2, h=HEADS)), s_free)
                elif kind == "norms":
                    qk, half = i % 2, i // 2
                    tell(dve.tensor_reduce(tops[:, 2 * qk + half:2 * qk + half + 1], misc[:], AX.X,
                                           ALU.max), s_free)
                    if i == 3:
                        for m in range(2):
                            link(dve.tensor_tensor(top2[:, m:m + 1], tops[:, 2 * m:2 * m + 1],
                                                   tops[:, 2 * m + 1:2 * m + 2], ALU.max))
                        link(dve.tensor_tensor(top2[:, 2:3], top2[:, 0:1], top2[:, 1:2], ALU.mult))
                        tell(dve.tensor_scalar(over[:], top2[:, 2:3], BOUND ** 2 * HD, None, ALU.is_gt),
                             s_over)
                elif kind == "count":
                    tell(dve.tensor_copy(flags[0:1, c:c + 1], misc[0:1, 0:1]), s_free)
                    tell_flag()
                elif kind == "project":
                    if i == 0:
                        dve.wait_ge(s_res, 16 * (c + 1))
                    r = res[:, 2 * i:2 * i + 2, :]
                    tell(dve.tensor_tensor(r, misc[:].rearrange("p (t d) -> p t d", t=2), r, ALU.add),
                         s_free)
                    for t in (2 * i, 2 * i + 1):
                        link(dve.bn_stats(stats[:, t, :], res[:, t, :]))
                        link(dve.bn_aggr(mv[:, t, :], stats[:, t, :]))
                    if i == 3:
                        tell(dve.tensor_scalar(lnt[:, 0, :], mv[:, :, 1], EPS, None, ALU.add), s_var)
                elif kind == "turn":
                    tell(dve.tensor_copy(x1T[:].rearrange("p t k n -> p (t k n)"), misc[:]), s_free)
                elif kind == "router":
                    tell(dve.tensor_tensor(
                        rt[:, 0, 2 * i:2 * i + 2, :],
                        misc[:, 0:2 * EXPERTS].rearrange("p (t e) -> p t e", e=EXPERTS),
                        br[:].unsqueeze(1).to_broadcast((P, 2, EXPERTS)), ALU.add), s_free)
                    if i == 3:
                        link(dve.tensor_reduce(rs[:, 0, :], rt[:, 0], AX.X, ALU.max))
                        tell(dve.tensor_tensor(rt[:, 1], rt[:, 0], wide(rs[:, 0, :]), ALU.subtract),
                             s_logit)
                elif kind == "place":
                    tell(dve.tensor_copy(rt[:, 6].rearrange("p t e -> p (t e)"),
                                         misc[:, 0:TB * EXPERTS]), s_free)
                    slots(c)

            def tell_flag():
                tell(dve.memset(top2[:, 0:1], 0.0), s_flag)

            def wide(a):
                return a.unsqueeze(2).to_broadcast((P, TB, EXPERTS))

            def norm(b):
                dve.wait_ge(s_rstd, b + 1)
                newton(dve, link, lnt)
                for t in range(TB):
                    ins = dve.tensor_scalar(res[:, t, :], res[:, t, :], mv[:, t, 0:1], lnt[:, 4, t:t + 1],
                                            ALU.subtract, ALU.mult)
                    if t < TB - 1:
                        link(ins)
                tell(ins, s_x1)

            def top_two(b):
                dve.wait_ge(s_gexp, b + 1)
                link(dve.tensor_reduce(rs[:, 1, :], rt[:, 1], AX.X, ALU.add))
                link(dve.reciprocal(rs[:, 2, :], rs[:, 1, :]))
                link(dve.tensor_tensor(rt[:, 2], rt[:, 1], wide(rs[:, 2, :]), ALU.mult))
                for k in range(2):
                    g, pick = rt[:, 2 + k], rt[:, 4 + k]
                    link(dve.tensor_reduce(rs[:, 3 + k, :], g, AX.X, ALU.max))
                    link(dve.tensor_tensor(rt[:, 7], g, wide(rs[:, 3 + k, :]), ALU.is_equal))
                    link(dve.tensor_tensor(rt[:, 7], rt[:, 7], rev[:], ALU.mult))
                    link(dve.tensor_reduce(rs[:, 5, :], rt[:, 7], AX.X, ALU.max))
                    link(dve.tensor_tensor(pick, rt[:, 7], wide(rs[:, 5, :]), ALU.is_equal))
                    if k == 0:
                        link(dve.scalar_tensor_tensor(rt[:, 3].rearrange("p t e -> p (t e)"),
                                                      pick.rearrange("p t e -> p (t e)"), -4.0,
                                                      g.rearrange("p t e -> p (t e)"),
                                                      ALU.mult, ALU.add))
                tell(dve.tensor_tensor(mask[:], rt[:, 4], rt[:, 5], ALU.add), s_mask)

            def slots(b):
                with nc.allow_low_precision(reason="counts of tiles, below 256: exact"):
                    link(dve.tensor_reduce(rs[:, 6, :], mask[:].rearrange("p t e -> p e t"), AX.X, ALU.add))
                    link(dve.tensor_tensor(before[:], before[:], rs[:, 6, :], ALU.add))
                link(dve.tensor_scalar(rt[:, 8], rt[:, 6], float(CAP), None, ALU.is_le))
                link(dve.tensor_tensor(rt[:, 9], rt[:, 6], slot_base[:], ALU.add))
                for k in range(2):
                    link(dve.tensor_tensor(rt[:, 10], rt[:, 4 + k], rt[:, 8], ALU.mult))
                    link(dve.tensor_reduce(rs[:, 7, :], rt[:, 10], AX.X, ALU.add))
                    link(dve.tensor_tensor(rt[:, 11], rt[:, 10], rt[:, 9], ALU.mult))
                    link(dve.tensor_reduce(rs[:, 8, :], rt[:, 11], AX.X, ALU.add))
                    link(dve.tensor_tensor(gate_w[:, TB * b:TB * (b + 1), k], rs[:, 3 + k, :], rs[:, 7, :],
                                           ALU.mult))
                    link(dve.tensor_copy(gather_idx[:, TB * b:TB * (b + 1), k], rs[:, 8, :]))
                    link(dve.tensor_scalar(rs[:, 9, :], rs[:, 7, :], -float(OOB), float(OOB),
                                           ALU.mult, ALU.add))
                    if k == 0:
                        if b:
                            dve.wait_ge(s_scat, 16 * 2 * TB * b)
                    ins = dve.tensor_tensor(scatter_idx[:, k, :], rs[:, 8, :], rs[:, 9, :], ALU.add)
                    if k == 0:
                        link(ins)
                tell(ins, s_idx)

            def read_outputs(blk):
                dve.wait_ge(s_pv, TB * (blk + 1))
                if blk:
                    dve.wait_ge(s_norm, blk)
                tell(dve.tensor_copy(oraw[:], opsum[:]), s_ofree)

            def sums(blk):
                link(dve.stream_shuffle(oden[:], oraw[:], [HD] * 32))
                tell(dve.reciprocal(oden[:], oden[:]), s_sums)

            def general_maxima(grp):
                dve.wait_ge(s_flag, grp // 2 + 1)
                flag = dve.value_load(flags[0:1, grp // 2:grp // 2 + 1], min_val=0, max_val=P)
                with dve.If(flag > 0):
                    full, free = (GEN + 1) * grp, (GEN + 2) * grp
                    for m in range(GEN):
                        dve.wait_ge(g_full, full + m + 1)
                        dve.tensor_reduce(gmax[:, m:m + 1], misc[:], AX.X, ALU.max).then_inc(g_free, 1)
                    dve.wait_ge(g_free, free + GEN)
                    dve.tensor_reduce(gneg[:], gmax[:].rearrange("p (m h) -> p m h", h=2), AX.X, ALU.max,
                                      negate=True).then_inc(g_free, 1)
                    dve.wait_ge(g_full, full + GEN + 1)
                    dve.tensor_copy(grow[:], misc[0:GH * TB, 0:P]).then_inc(g_free, 1)
                    dve.wait_ge(g_free, free + GEN + 2)
                with dve.Else():
                    dve.sem_inc(g_free, GEN + 2)

            key_angles(0)
            for s in range(first, last + 1):
                if 0 < s <= NSTEP and s % TB == 0:
                    read_outputs(s // TB - 1)
                if 0 <= s < NSTEP and s % STEPS == 0:
                    general_maxima(s // STEPS)
                for job in jobs_at(s):
                    read_out(job)
                for job in jobs_at(s - 2):
                    if job[0] == "qk":
                        split_unit(*job[1:])
                if s == first + 2:
                    set_up()
                    key_angles(1)
                if (b := tail_at(s, "norm")) is not None:
                    norm(b)
                if (b := tail_at(s, "top")) is not None:
                    top_two(b)
                if TB <= s - 2 <= NSTEP and (s - 2) % TB == 0:
                    sums((s - 2) // TB - 1)


def newton(dve, link, lnt):
    link(dve.tensor_tensor(lnt[:, 3, :], lnt[:, 2, :], lnt[:, 2, :], ALU.mult))
    link(dve.tensor_tensor(lnt[:, 3, :], lnt[:, 3, :], lnt[:, 0, :], ALU.mult))
    link(dve.tensor_scalar(lnt[:, 3, :], lnt[:, 3, :], -0.5, 1.5, ALU.mult, ALU.add))
    link(dve.tensor_tensor(lnt[:, 4, :], lnt[:, 2, :], lnt[:, 3, :], ALU.mult))


def experts(nc, w1_d, b1_d, w2_d, b2_d, disp_d, x1_d, eo_d, ident, gather_idx, gate_w, out):
    NT = BATCH * TB
    with ExitStack() as ctx:
        sb = lambda name, shape, dt=F32: ctx.enter_context(nc.sbuf_tensor(name, shape, dt))
        sem = lambda name: ctx.enter_context(nc.semaphore(name))
        w1 = [sb(f"w1_{i}", [P, KC, HIDDEN]) for i in range(2)]
        w2 = [sb(f"w2_{i}", [P, HK, DIM]) for i in range(2)]
        b1 = sb("b1", [P, EXPERTS, HK])
        b2 = sb("b2", [P, EXPERTS, DIM])
        rows = [sb(f"rows{i}", [P, ST, DIM]) for i in range(2)]
        xe = [sb(f"xe{i}", [P, KC, CAP]) for i in range(2)]
        hid = [sb(f"hid{i}", [P, HK, CAP]) for i in range(1)]
        eo = [sb(f"eo{i}", [P, ST, DIM]) for i in range(2)]
        NR = 4
        got = [sb(f"got{i}", [P, 2, DIM]) for i in range(NR)]
        x1 = [sb(f"x1_{i}", [P, TB, DIM]) for i in range(2)]
        stats = sb("stats2", [P, TB, 6])
        mv = sb("mv2", [P, TB, 2])
        lnt = sb("lnt2", [P, 5, TB])
        hp = [ctx.enter_context(nc.psum_tensor(f"hp{i}", [P, 2, HALF], F32)) for i in range(2)]
        yp = [ctx.enter_context(nc.psum_tensor(f"yp{i}", [P, HALF], F32)) for i in range(2)]
        tp = [ctx.enter_context(nc.psum_tensor(f"tp{i}", [P, HALF], F32)) for i in range(2)]

        s_bias = sem("s_bias")
        s_w = [sem(f"s_w{i}") for i in range(2)]
        s_rows = [sem(f"s_rows{i}") for i in range(2)]
        s_turn, s_turned = sem("s_turn"), sem("s_turned")
        s_h, s_gelu = sem("s_h"), sem("s_gelu")
        s_y, s_yout = sem("s_y"), sem("s_yout")
        s_eo = [sem(f"s_eo{i}") for i in range(2)]
        s_got = [sem(f"s_got{i}") for i in range(NR)]
        s_x1l = [sem(f"s_x1l{i}") for i in range(2)]
        s_used = sem("s_used")
        s_var, s_rstd, s_done, s_out = sem("s_var2"), sem("s_rstd2"), sem("s_done"), sem("s_out")
        s_chain, s_actchain = sem("s_chain2"), sem("s_actchain2")
        block = ctx.enter_context(nc.Block())

        @block.sync
        def _(sp):
            def load(e):
                p = e % 2
                if e >= 2:
                    sp.wait_ge(s_y, ST * (e - 1))
                sp.dma_start(rows[p][:], disp_d[e * CAP:(e + 1) * CAP].rearrange("(t p) d -> p t d", p=P)
                             ).then_inc(s_rows[p], 16)
                sp.dma_start(w1[p][:], w1_d[e].rearrange("(k p) n -> p k n", p=P)).then_inc(s_w[p], 16)
                sp.dma_start(w2[p][:], w2_d[e].rearrange("(k p) n -> p k n", p=P)).then_inc(s_w[p], 16)

            load(0)
            sp.dma_start(b1[:], b1_d).then_inc(s_bias, 16)
            sp.dma_start(b2[:].rearrange("p e d -> p (e d)"), b2_d.to_broadcast((P, EXPERTS * DIM))
                         ).then_inc(s_bias, 16)
            load(1)
            for e in range(EXPERTS):
                if e >= 1 and e + 1 < EXPERTS:
                    load(e + 1)
                sp.wait_ge(s_yout, ST * (e + 1))
                sp.dma_start(eo_d[e * CAP:(e + 1) * CAP].rearrange("(t p) d -> p t d", p=P),
                             eo[e % 2][:]).then_inc(s_eo[e % 2], 16)
                if e < 2:
                    sp.dma_start(x1[e][:], x1_d[e * SEQ:(e + 1) * SEQ].rearrange("(t p) d -> p t d", p=P)
                                 ).then_inc(s_x1l[e], 16)
            for b in range(BATCH):
                sp.wait_ge(s_done, b + 1)
                sp.dma_start(out[b].rearrange("(t p) d -> p t d", p=P), x1[b % 2][:]).then_inc(s_out, 16)
                if b + 2 < BATCH:
                    sp.wait_ge(s_out, 16 * (b + 1))
                    sp.dma_start(x1[b % 2][:],
                                 x1_d[(b + 2) * SEQ:(b + 3) * SEQ].rearrange("(t p) d -> p t d", p=P)
                                 ).then_inc(s_x1l[b % 2], 16)
            sp.wait_ge(s_out, 16 * BATCH)

        @block.gpsimd
        def _(pool):
            for i in range(2):
                pool.wait_ge(s_eo[i], 16 * EXPERTS // 2)
            for t in range(NT):
                if t >= NR:
                    pool.wait_ge(s_used, t - NR + 1)
                for k in range(2):
                    pool.indirect_dma_start(
                        got[t % NR][:, k, :], None, eo_d,
                        bass.IndirectOffsetOnAxis(ap=gather_idx[:, t, k:k + 1], axis=0),
                        bounds_check=SLOTS - 1, oob_is_err=False).then_inc(s_got[t % NR], 16)

        @block.tensor
        def _(pe):
            turns = 0

            def turn(e):
                nonlocal turns
                pe.wait_ge(s_rows[e % 2], 16 * (e // 2 + 1))
                for t in range(ST):
                    if turns >= 2:
                        pe.wait_ge(s_turned, turns - 1)
                    for k in range(KC):
                        ins = pe.transpose(tp[turns % 2][:, P * k:P * (k + 1)],
                                           rows[e % 2][:, t, P * k:P * (k + 1)], ident[:])
                    ins.then_inc(s_turn, 1)
                    turns += 1

            turn(0)
            for e in range(EXPERTS):
                pe.wait_ge(s_w[e % 2], 32 * (e // 2 + 1))
                pe.wait_ge(s_turned, ST * (e + 1))
                for m in range(HK):
                    n = HK * e + m
                    if n >= 2:
                        pe.wait_ge(s_gelu, n - 1)
                    for k in range(KC):
                        for h in range(2):
                            ins = pe.matmul(hp[n % 2][:, h, 0:CH], w1[e % 2][:, k, P * m:P * (m + 1)],
                                            xe[e % 2][:, k, CH * h:CH * (h + 1)],
                                            start=k == 0, stop=k == KC - 1)
                    ins.then_inc(s_h, 1)
                if e + 1 < EXPERTS:
                    turn(e + 1)
                pe.wait_ge(s_gelu, HK * (e + 1))
                for t in range(ST):
                    n = ST * e + t
                    if n >= 2:
                        pe.wait_ge(s_yout, n - 1)
                    for m in range(HK):
                        ins = pe.matmul(yp[n % 2][:, 0:DIM], hid[0][:, m, P * t:P * (t + 1)],
                                        w2[e % 2][:, m, :], start=m == 0, stop=m == HK - 1)
                    ins.then_inc(s_y, 1)

        @block.scalar
        def _(act):
            done = [0]
            act.wait_ge(s_bias, 32)
            for e in range(EXPERTS):
                for m in range(HK):
                    n = HK * e + m
                    act.wait_ge(s_h, n + 1)
                    if m == 0 and e:
                        act.wait_ge(s_y, ST * e)
                    act.activation(hid[0][:, m, :].rearrange("p (h n) -> p h n", h=2), hp[n % 2][:, :, 0:CH],
                                   ACT.Gelu, bias=b1[:, e, m:m + 1]).then_inc(s_gelu, 1)
            act.preload_act_table_set("natural_log_exp_and_others")
            for b in range(BATCH):
                act.wait_ge(s_var, b + 1)
                act.activation(lnt[:, 1, :], lnt[:, 0, :], ACT.Ln).then_inc(s_actchain, 1)
                act.wait_ge(s_actchain, b + 1)
                act.activation(lnt[:, 2, :], lnt[:, 1, :], ACT.Exp, scale=-0.5).then_inc(s_rstd, 1)

        @block.vector
        def _(dve):
            links = [0]

            def link(ins):
                links[0] += 1
                ins.then_inc(s_chain, 1)
                dve.wait_ge(s_chain, links[0])

            turns = 0

            def turned(e):
                nonlocal turns
                for t in range(ST):
                    if t == 0 and e >= 2:
                        dve.wait_ge(s_h, HK * (e - 1))
                    dve.wait_ge(s_turn, turns + 1)
                    dve.tensor_copy(xe[e % 2][:, :, P * t:P * (t + 1)],
                                    tp[turns % 2][:, 0:DIM].rearrange("p (k n) -> p k n", k=KC)
                                    ).then_inc(s_turned, 1)
                    turns += 1

            turned(0)
            dve.wait_ge(s_bias, 32)
            for e in range(EXPERTS):
                if e + 1 < EXPERTS:
                    turned(e + 1)
                if e >= 2:
                    dve.wait_ge(s_eo[e % 2], 16 * (e // 2))
                for t in range(ST):
                    n = ST * e + t
                    dve.wait_ge(s_y, n + 1)
                    dve.tensor_tensor(eo[e % 2][:, t, :], yp[n % 2][:, 0:DIM], b2[:, e, :], ALU.add
                                      ).then_inc(s_yout, 1)
            for b in range(BATCH):
                dve.wait_ge(s_x1l[b % 2], 16 * (b // 2 + 1))
                for t in range(TB):
                    n = TB * b + t
                    dve.wait_ge(s_got[n % NR], 32 * (n // NR + 1))
                    row = x1[b % 2][:, t, :]
                    link(dve.scalar_tensor_tensor(row, got[n % NR][:, 0, :], gate_w[:, n, 0:1], row,
                                                  ALU.mult, ALU.add))
                    dve.scalar_tensor_tensor(row, got[n % NR][:, 1, :], gate_w[:, n, 1:2], row,
                                             ALU.mult, ALU.add).then_inc(s_used, 1)
                    dve.wait_ge(s_used, n + 1)
                    link(dve.bn_stats(stats[:, t, :], row))
                    link(dve.bn_aggr(mv[:, t, :], stats[:, t, :]))
                dve.tensor_scalar(lnt[:, 0, :], mv[:, :, 1], EPS, None, ALU.add).then_inc(s_var, 1)
                dve.wait_ge(s_var, b + 1)
                dve.wait_ge(s_rstd, b + 1)
                newton(dve, link, lnt)
                for t in range(TB):
                    ins = dve.tensor_scalar(x1[b % 2][:, t, :], x1[b % 2][:, t, :], mv[:, t, 0:1],
                                            lnt[:, 4, t:t + 1], ALU.subtract, ALU.mult)
                    if t < TB - 1:
                        link(ins)
                ins.then_inc(s_done, 1)
                dve.wait_ge(s_done, b + 1)


def kernel(L0_attn_x, L0_attn_wq, L0_attn_wk, L0_attn_wv, L0_attn_wo, L0_attn_pope_bias,
           L0_ffn_router_w, L0_ffn_router_b, L0_ffn_w1, L0_ffn_b1, L0_ffn_w2, L0_ffn_b2):
    import numpy as np
    import concourse.bacc as bacc
    from concourse.bass_utils import run_bass_kernel_spmd

    def parts(a):
        a = np.asarray(a)
        return np.ascontiguousarray(a.reshape(-1, P, a.shape[1]).transpose(1, 0, 2))

    x = np.asarray(L0_attn_x)
    pos = np.arange(SEQ, dtype=np.float32)
    inv = (10000.0 ** -(np.arange(HD) / HD)).astype(np.float32)
    angle = (pos[None, :] * inv[:, None]).astype(np.float32).astype(np.float64)
    trig = np.stack([np.cos(angle), np.sin(angle)], axis=1).astype(np.float32)
    e = np.arange(EXPERTS, dtype=np.float32)
    arrays = {
        "x": np.ascontiguousarray(x.reshape(BATCH, TB, P, DIM).transpose(0, 2, 1, 3)),
        "xT": np.ascontiguousarray(x.reshape(BATCH, SEQ, KC, P).transpose(0, 3, 2, 1)),
        "wq": parts(np.asarray(L0_attn_wq).T),
        "wk": parts(np.asarray(L0_attn_wk).T),
        "wv": parts(np.asarray(L0_attn_wv).T),
        "wo": parts(np.asarray(L0_attn_wo).T),
        "bias": np.ascontiguousarray(np.asarray(L0_attn_pope_bias).reshape(KC, P).T),
        "wr": parts(L0_ffn_router_w),
        "br": np.asarray(L0_ffn_router_b).reshape(1, EXPERTS),
        "w1": np.ascontiguousarray(L0_ffn_w1),
        "b1": np.ascontiguousarray(np.asarray(L0_ffn_b1).reshape(EXPERTS, HK, P).transpose(2, 0, 1)),
        "w2": np.ascontiguousarray(L0_ffn_w2),
        "b2": np.ascontiguousarray(np.asarray(L0_ffn_b2).reshape(1, EXPERTS * DIM)),
        "trig": np.ascontiguousarray(np.tile(trig, (P // HD, 1, 1))),
        "ident": np.eye(P, dtype=np.float32),
        "tri": np.triu(np.ones((P, P), np.float32)),
        "blocks": np.kron(np.eye(P // HD, dtype=np.float32), np.ones((HD, HD), np.float32)),
        "rev": np.tile(EXPERTS - e, (P, TB)).astype(np.float32),
        "base": np.tile(e * CAP - 1, (P, TB)).astype(np.float32),
    }
    nc = bacc.Bacc("TRN2", target_bir_lowering=False, num_devices=1)
    args = [nc.dram_tensor(f"in_{n}", a.shape, mybir.dt.from_np(a.dtype), kind="ExternalInput").ap()
            for n, a in arrays.items()]
    out = nc.dram_tensor("out", (BATCH, SEQ, DIM), F32, kind="ExternalOutput").ap()
    build(nc, *args, out)
    r = run_bass_kernel_spmd(nc, [{f"in_{n}": a for n, a in arrays.items()}], core_ids=[0])
    return r.results[0]["out"]
```

```python
from contextlib import ExitStack

import concourse.bass as bass
from concourse import mybir

F32 = mybir.dt.float32
F32R = mybir.dt.float32r
BF16 = mybir.dt.bfloat16
I32 = mybir.dt.int32
ALU = mybir.AluOpType
ACT = mybir.ActivationFunctionType
AX = mybir.AxisListType

P = 128
BATCH, SEQ, DIM, HEADS = 4, 1024, 256, 16
HD = DIM // HEADS
EXPERTS, HIDDEN = 8, 1024
TOKENS = BATCH * SEQ
CAP = -(-TOKENS * 5 // (EXPERTS * 4))
SLOTS = EXPERTS * CAP
EPS = 1e-5
PI = 3.1415927410125732

KC = DIM // P
TB = SEQ // P
GH = 4
GROUPS = HEADS // GH
HALF = SEQ // 2
STEPS = 2 * TB
NG = BATCH * GROUPS
NSTEP = NG * STEPS
ROWS = 3 * 2 * HD
BOUND = 60.0
ST = CAP // P
HK = HIDDEN // P
CH = CAP // 2
GATES = DIM
TOKEN = DIM + EXPERTS
WIDE = TOKEN + 1
OOB = 2 * SLOTS


def misc_schedule():
    at = {}

    def put(s, job):
        at.setdefault(s, []).append(job)

    for i in range(4):
        put(-13 + 3 * i, ("qk", 0, i))
        put(-12 + 3 * i, ("v", 0, i))
        put(-10 + 3 * i, ("norms", 0, i))
    put(-1, ("count", 0))
    for grp in range(0, NG - 2, 2):
        c, s0 = grp // 2 + 1, STEPS * grp
        for i in range(4):
            put(s0 + (2, 5, 10, 13)[i], ("qk", c, i))
            put(s0 + (5, 9, 14, 17)[i], ("norms", c, i))
        put(s0 + 18, ("count", c))
        if grp % GROUPS == 2:
            for i in range(4):
                put(s0 + STEPS + (4, 7, 12, 15)[i], ("v", grp // GROUPS + 1, i))
    for b in range(BATCH):
        s0, t = STEPS * GROUPS * (b + 1), TAIL[b == BATCH - 1]
        for i in range(4):
            put(s0 + t["project"][i], ("project", b, i))
            put(s0 + t["turn"][i], ("turn", b, i))
            put(s0 + t["router"][i], ("router", b, i))
        put(s0 + t["place"], ("place", b))
    return at


TAIL = {
    False: dict(project=(8, 9, 11, 12), rstd=14, norm=15, turn=(19, 21, 23, 26), router=(20, 22, 25, 28),
                exp=29, top=30, place=31),
    True: dict(project=(4, 5, 6, 7), rstd=8, norm=9, turn=(10, 12, 14, 16), router=(11, 13, 15, 17),
               exp=18, top=19, place=20),
}


def build(nc, x_d, xT_d, wq_d, wk_d, wv_d, wo_d, bias_d, wr_d, br_d, w1_d, b1_d, w2_d, b2_d,
          trig_d, ident_d, tri_d, blocks_d, rev_d, base_d, blank_d, number_d, tile_d, out):
    jobs = misc_schedule()
    first, last = min(jobs), NSTEP + TAIL[True]["place"] + 1
    number, n = {}, 0
    for s in range(first, last + 1):
        for job in jobs.get(s, ()):
            number[job] = n
            n += 1

    split_d = nc.dram_tensor("split_scratch", (2, BATCH, 2, HEADS, 2 * HD, SEQ), F32).ap()
    disp_d = nc.dram_tensor("dispatched", (SLOTS, WIDE), F32).ap()
    sum_d = nc.dram_tensor("sum_scratch", (TOKENS + CAP, DIM), F32).ap()

    with ExitStack() as both:
        sb2 = lambda name, shape, dt=F32: both.enter_context(nc.sbuf_tensor(name, shape, dt))
        ident = sb2("ident", [P, P])
        area_k = sb2("area_k", [P, KC * 2 * SEQ])
        area_q = sb2("area_q", [P, GH, SEQ], F32R)
        area_s = sb2("area_s", [P, 2 * 2 * 2 * HALF], F32R)
        areas = (area_k, area_q, area_s)
        attention(nc, jobs, number, first, last, x_d, xT_d, wq_d, wk_d, wv_d, wo_d, bias_d, wr_d,
                  br_d, trig_d, ident_d, tri_d, blocks_d, rev_d, base_d, blank_d, number_d, w1_d,
                  w2_d, split_d, disp_d, sum_d, ident, areas)
        experts(nc, w1_d, b1_d, w2_d, b2_d, tile_d, disp_d, sum_d, ident, areas, out)


def weight_views(areas):
    area_k, area_q, area_s = areas
    raw1 = area_k[:, 0:KC * HIDDEN].rearrange("p (k n) -> p k n", k=KC)
    raw2 = area_k[:, KC * HIDDEN:].rearrange("p (k n) -> p k n", k=HK)
    w1s = area_s[:].rearrange("p (s k n) -> p s k n", s=2, k=KC)
    w2s = area_q[:].rearrange("p (s a) n -> p s (a n)", s=2).rearrange("p s (k n) -> p s k n", k=HK)
    return raw1, raw2, w1s, w2s


def attention(nc, jobs, number, first, last, x_d, xT_d, wq_d, wk_d, wv_d, wo_d, bias_d, wr_d, br_d,
              trig_d, ident_d, tri_d, blocks_d, rev_d, base_d, blank_d, number_d, w1_d, w2_d,
              split_d, disp_d, sum_d, ident, areas):
    with ExitStack() as ctx:
        sb = lambda name, shape, dt=F32: ctx.enter_context(nc.sbuf_tensor(name, shape, dt))
        sem = lambda name: ctx.enter_context(nc.semaphore(name))

        area_k, area_q, area_s = areas
        qtrig = sb("qtrig", [P, 2, SEQ])[:]
        ktrig = area_k[:].rearrange("p (k t n) -> p k t n", k=KC, t=2)
        raw1, raw2, w1s, w2s = weight_views(areas)
        wqkv = sb("wqkv", [P, 3, KC, DIM])
        woT = sb("woT", [P, KC, DIM])
        wr = sb("wr", [P, KC, EXPERTS])
        br = sb("br", [P, EXPERTS])
        tri_f = sb("tri_f", [P, P])
        tri = sb("tri", [P, P], BF16)
        ones = sb("ones", [P, P], BF16)
        blocks_f = sb("blocks_f", [P, P])
        blocks = sb("blocks", [P, P], BF16)
        square = sb("square", [P, HALF], BF16)
        ones_col = sb("ones_col", [P, 1])
        rev = sb("rev", [P, TB, EXPERTS])
        slot_base = sb("slot_base", [P, TB, EXPERTS])
        blank = sb("blank", [P, WIDE])
        token_no = sb("token_no", [P, BATCH * TB])
        ang = sb("ang", [P, 6, KC])
        xT = sb("xT", [P, KC, SEQ])[:]
        raw = sb("raw", [P, HALF])
        soft = sb("soft", [P, HALF])
        emb = sb("emb", [P, 2, HALF])
        split = [area_s[:, 4 * HALF * i:4 * HALF * (i + 1)].rearrange("p (s t n) -> p s t n", s=2, t=2)
                 for i in range(2)]
        tops = sb("tops", [P, 4])
        top2 = sb("top2", [P, 3])
        over = sb("over", [P, 1])
        flags = sb("flags", [1, NG // 2], I32)
        qst = [area_q[0:ROWS + 1], sb("qst1", [ROWS + 1, GH, SEQ], F32R)[:]]
        kst = [sb(f"kst{i}", [ROWS + 1, GH, SEQ], F32R) for i in range(2)]
        val = [sb(f"val{i}", [P, TB, HEADS, HD + 1]) for i in range(2)]
        NPB, NSB = 4, 3
        prob = [sb(f"prob{i}", [P, 2 * HALF]) for i in range(NPB)]
        oraw = sb("oraw", [P, HALF])
        oden = sb("oden", [P, HALF])
        onorm = sb("onorm", [P, HALF])
        aT = sb("aT", [P, KC, SEQ])
        res = sb("res", [P, TB, WIDE])
        stats = sb("stats", [P, TB, 6])
        mv = sb("mv", [P, TB, 2])
        lnt = sb("lnt", [P, 5, TB])
        x1T = sb("x1T", [P, 2, KC, P])
        rt = sb("rt", [P, 12, TB, EXPERTS])
        rs = sb("rs", [P, 16, TB])
        mask = sb("mask", [P, TB, EXPERTS], BF16)
        before = sb("before", [P, EXPERTS], BF16)
        scatter_idx = sb("scatter_idx", [P, 2, TB], I32)
        gmax = sb("gmax", [P, 2 * GH * TB])
        gneg = sb("gneg", [P, GH * TB])
        grow = sb("grow", [GH * TB, P], F32R)

        spsum = [ctx.enter_context(nc.psum_tensor(f"spsum{i}", [P, 2, HALF], F32)) for i in range(NSB)]
        opsum = ctx.enter_context(nc.psum_tensor("opsum", [P, HALF], F32))
        misc = ctx.enter_context(nc.psum_tensor("misc", [P, HALF], F32))

        s_wqk, s_trig, s_wv = sem("s_wqk"), sem("s_trig"), sem("s_wv")
        s_setup, s_sums = sem("s_setup"), sem("s_sums")
        s_raw, s_hi = sem("s_raw"), sem("s_hi")
        s_const, s_xT, s_res, s_zero = sem("s_const"), sem("s_xT"), sem("s_res"), sem("s_zero")
        s_blank, s_w0, s_whi = sem("s_blank"), sem("s_w0"), sem("s_whi")
        s_chain = sem("s_chain")
        s_actchain = sem("s_actchain")
        s_angle, s_sin = sem("s_angle"), sem("s_sin")
        s_full, s_free = sem("s_misc_full"), sem("s_misc_free")
        s_abs, s_soft = sem("s_abs"), sem("s_soft")
        s_split = sem("s_split")
        s_store = [sem(f"s_store{i}") for i in range(4)]
        s_square, s_over, s_flag = sem("s_square"), sem("s_over"), sem("s_flag")
        s_fill = [sem(f"s_fill{i}") for i in range(2)]
        s_score, s_exp, s_pv = sem("s_score"), sem("s_exp"), sem("s_pv")
        s_ofree, s_norm, s_aT = sem("s_ofree"), sem("s_onorm"), sem("s_aT")
        s_var, s_rstd, s_x1 = sem("s_var"), sem("s_rstd"), sem("s_x1")
        s_logit, s_gexp, s_mask, s_idx = sem("s_logit"), sem("s_gexp"), sem("s_mask"), sem("s_idx")
        s_scat, s_x1d = sem("s_scat"), sem("s_x1d")
        g_full, g_free, g_row = sem("s_gen_full"), sem("s_gen_free"), sem("s_gen_row")
        GEN = 2 * GH * TB

        NCONST = 9
        block = ctx.enter_context(nc.Block())

        def jobs_at(s):
            return jobs.get(s, ())

        def tail_at(s, what):
            for b in range(BATCH):
                if s == STEPS * GROUPS * (b + 1) + TAIL[b == BATCH - 1][what]:
                    return b
            return None

        @block.sync
        def _(sp):
            sp.dma_start(wqkv[:, 0], wq_d).then_inc(s_wqk, 16)
            sp.dma_start(xT, xT_d[0]).then_inc(s_xT, 16)
            sp.dma_start(wqkv[:, 1], wk_d).then_inc(s_wqk, 16)
            sp.dma_start(ang[:, 0, :], bias_d).then_inc(s_trig, 16)
            sp.dma_start(qtrig, trig_d).then_inc(s_trig, 16)
            sp.dma_start(blank[:], blank_d).then_inc(s_blank, 16)
            sp.dma_start(wqkv[:, 2], wv_d).then_inc(s_wv, 16)
            sp.dma_start(woT[:], wo_d).then_inc(s_const, 16)
            sp.dma_start(wr[:], wr_d).then_inc(s_const, 16)
            sp.dma_start(br[:], br_d.to_broadcast((P, EXPERTS))).then_inc(s_const, 16)
            sp.dma_start(ident[:], ident_d).then_inc(s_const, 16)
            sp.dma_start(tri_f[:], tri_d).then_inc(s_const, 16)
            sp.dma_start(blocks_f[:], blocks_d).then_inc(s_const, 16)
            sp.dma_start(rev[:].rearrange("p t e -> p (t e)"), rev_d).then_inc(s_const, 16)
            sp.dma_start(token_no[:], number_d).then_inc(s_const, 16)
            sp.dma_start(slot_base[:].rearrange("p t e -> p (t e)"), base_d).then_inc(s_const, 16)
            sp.dma_start(res[:, :, 0:DIM], x_d[0]).then_inc(s_res, 16)

            def fill(grp):
                b, h0, par = grp // GROUPS, GH * (grp % GROUPS), grp % 2
                for i in range(4):
                    sp.wait_ge(s_store[i], 32 * (grp // 2 + 1))
                if grp >= 2:
                    sp.wait_ge(s_score, 2 * STEPS * (grp - 1))
                for qk, stack, terms in ((0, qst, (0, 0, 1)), (1, kst, (0, 1, 0))):
                    for r, part in enumerate(terms):
                        sp.dma_start(stack[par][2 * HD * r:2 * HD * (r + 1)].bitcast(F32),
                                     split_d[qk, b, part, h0:h0 + GH].rearrange("h r n -> r h n")
                                     ).then_inc(s_fill[par], 16)
                sp.dma_start(qst[par][ROWS:ROWS + 1].bitcast(F32),
                             blank[0:GH * SEQ // DIM, 0:DIM]).then_inc(s_fill[par], 16)
                sp.wait_ge(s_flag, grp // 2 + 1)
                flag = sp.value_load(flags[0:1, grp // 2:grp // 2 + 1], min_val=0, max_val=P)
                with sp.If(flag > 0):
                    sp.wait_ge(g_free, (GEN + 2) * (grp + 1))
                    sp.wait_ge(s_fill[par], 112 * (grp // 2 + 1))
                    sp.dma_start(qst[par][ROWS:ROWS + 1].bitcast(F32),
                                 grow[:].bitcast(F32)).then_inc(g_row, 16)
                with sp.Else():
                    sp.sem_inc(g_row, 16)

            def gather_heads(blk):
                b, g, qh = blk // (2 * GROUPS), blk // 2 % GROUPS, blk % 2
                sp.wait_ge(s_norm, blk + 1)
                if b and blk % (2 * GROUPS) == 0:
                    sp.wait_ge(s_full, number["project", b - 1, 3] + 1)
                for j in range(GH):
                    r = (g % 2) * GH * HD + HD * j
                    sp.dma_start(aT[r:r + HD, g // 2, HALF * qh:HALF * (qh + 1)],
                                 onorm[32 * j:32 * j + HD, :]).then_inc(s_aT, 16)

            sp.wait_ge(s_blank, 16)
            fill(0)
            fill(1)
            for grp in range(NG):
                b = grp // GROUPS
                if grp:
                    gather_heads(2 * grp - 1)
                if 1 <= grp < NG - 1:
                    fill(grp + 1)
                if grp % GROUPS == 1 and b < BATCH - 1:
                    sp.wait_ge(s_full, number["qk", 2 * b + 1, 3] + 1)
                    sp.dma_start(xT, xT_d[b + 1]).then_inc(s_xT, 16)
                if grp % GROUPS == 3 and b:
                    sp.wait_ge(s_scat, 16 * 2 * TB * b)
                    sp.wait_ge(s_x1d, 16 * b)
                    sp.dma_start(res[:, :, 0:DIM], x_d[b]).then_inc(s_res, 16)
                gather_heads(2 * grp)
                if grp == NG - 2:
                    sp.wait_ge(s_hi, NG * 2)
                    sp.dma_start(raw1, w1_d[0].rearrange("(k p) n -> p k n", p=P)).then_inc(s_w0, 16)
                    sp.dma_start(raw2, w2_d[0].rearrange("(k p) n -> p k n", p=P)).then_inc(s_w0, 16)
            gather_heads(2 * NG - 1)

        @block.gpsimd
        def _(pool):
            def clear_slots():
                pool.wait_ge(s_blank, 16)
                pool.dma_start(disp_d.rearrange("(t p) d -> p t d", p=P),
                               blank[:].unsqueeze(1).to_broadcast((P, SLOTS // P, WIDE))
                               ).then_inc(s_zero, 16)
                pool.dma_start(sum_d[TOKENS:].rearrange("(t p) d -> p t d", p=P),
                               blank[:, 0:DIM].unsqueeze(1).to_broadcast((P, ST, DIM))
                               ).then_inc(s_zero, 16)

            def store_split(c, i):
                b, ct, qk, half = c // KC, c % KC, i % 2, i // 2
                u = 4 * c + i
                pool.wait_ge(s_raw, u + 1)
                if u:
                    pool.wait_ge(s_full, number["norms", (u - 1) // 4, (u - 1) % 4] + 1)
                pool.tensor_tensor(square[:], raw[:], raw[:], ALU.mult).then_inc(s_square, 1)
                pool.wait_ge(s_hi, u + 1)
                pool.tensor_tensor(split[u % 2][:, 1], emb[:], split[u % 2][:, 0].bitcast(F32),
                                   ALU.subtract).then_inc(s_split, 1)
                pool.wait_ge(s_split, u + 1)
                for part in range(2):
                    pool.dma_start(
                        split_d[qk, b, part, 8 * ct:8 * ct + 8, :, HALF * half:HALF * (half + 1)]
                        .rearrange("h (d t) n -> (h d) t n", t=2),
                        split[u % 2][:, part].bitcast(F32)).then_inc(s_store[i], 16)

            def scatter(b):
                pool.wait_ge(s_x1, b + 1)
                pool.dma_start(sum_d[b * SEQ:(b + 1) * SEQ].rearrange("(t p) d -> p t d", p=P),
                               res[:, :, 0:DIM]).then_inc(s_x1d, 16)
                pool.wait_ge(s_idx, b + 1)
                pool.wait_ge(s_zero, 32)
                for t in range(TB):
                    for k in range(2):
                        pool.indirect_dma_start(
                            disp_d, bass.IndirectOffsetOnAxis(ap=scatter_idx[:, k, t:t + 1], axis=0),
                            res[:, t, :], None, bounds_check=SLOTS - 1,
                            oob_is_err=False).then_inc(s_scat, 16)

            def normalise(blk):
                pool.wait_ge(s_sums, blk + 1)
                if blk:
                    pool.wait_ge(s_aT, 16 * GH * blk)
                pool.tensor_tensor(onorm[:], oraw[:], oden[:], ALU.mult).then_inc(s_norm, 1)

            def weight_remainders():
                for n, (raw_w, parts_w) in enumerate(((raw1, w1s), (raw2, w2s))):
                    pool.wait_ge(s_whi, n + 1)
                    pool.tensor_tensor(parts_w[:, 1], raw_w, parts_w[:, 0].bitcast(F32), ALU.subtract)

            for s in range(first, last + 1):
                for job in jobs_at(s - 2):
                    if job[0] == "qk":
                        store_split(*job[1:])
                if s == 0:
                    clear_slots()
                if s == NSTEP + 3:
                    weight_remainders()
                if TB <= s - 2 <= NSTEP and (s - 2) % TB == 0:
                    normalise((s - 2) // TB - 1)
                for job in jobs_at(s):
                    if job[0] == "place":
                        scatter(job[1])
            pool.wait_ge(s_scat, 16 * 2 * TB * BATCH)
            pool.wait_ge(s_x1d, 16 * BATCH)

        @block.scalar
        def _(act):
            done = [0]

            def chained(ins):
                done[0] += 1
                ins.then_inc(s_actchain, 1)
                act.wait_ge(s_actchain, done[0])

            act.wait_ge(s_angle, 1)
            act.activation(ang[:, 3:5, :], ang[:, 1:3, :], ACT.Sin).then_inc(s_sin, 1)
            act.preload_act_table_set("natural_log_exp_and_others")

            def softplus(u):
                act.wait_ge(s_abs, u + 1)
                chained(act.activation(soft[:], soft[:], ACT.Exp))
                act.activation(soft[:], soft[:], ACT.Ln, bias=1.0).then_inc(s_soft, 1)

            def rstd_guess(b):
                act.wait_ge(s_var, b + 1)
                chained(act.activation(lnt[:, 1, :], lnt[:, 0, :], ACT.Ln))
                act.activation(lnt[:, 2, :], lnt[:, 1, :], ACT.Exp, scale=-0.5).then_inc(s_rstd, 1)

            def weight_halves():
                act.wait_ge(s_w0, 32)
                for i in range(4):
                    act.wait_ge(s_store[i], 32 * NG // 2)
                act.copy(w1s[:, 0], raw1).then_inc(s_whi, 1)
                act.wait_ge(s_score, 2 * STEPS * (NG - 1))
                act.copy(w2s[:, 0], raw2).then_inc(s_whi, 1)

            def gates_exp(b):
                act.wait_ge(s_logit, b + 1)
                act.activation(rt[:, 1], rt[:, 1], ACT.Exp).then_inc(s_gexp, 1)

            for s in range(first, last + 1):
                if 0 <= s < NSTEP:
                    for u in (2 * s, 2 * s + 1):
                        act.wait_ge(s_score, u + 1)
                        if u >= NPB:
                            act.wait_ge(s_pv, (u - NPB) // 2 + 1)
                        act.activation(prob[u % NPB][:], spsum[u % NSB][:].rearrange("p a n -> p (a n)"),
                                       ACT.Exp, scale=HD ** -0.5).then_inc(s_exp, 1)
                for job in jobs_at(s - 1):
                    if job[0] == "qk":
                        softplus(4 * job[1] + job[2])
                if s == NSTEP + 3:
                    weight_halves()
                if (b := tail_at(s, "rstd")) is not None:
                    rstd_guess(b)
                if (b := tail_at(s, "exp")) is not None:
                    gates_exp(b)

        @block.tensor
        def _(pe):
            def begin(job):
                if number[job]:
                    pe.wait_ge(s_free, number[job])

            def run(job):
                kind, c, i = (*job, 0)[:3]
                begin(job)
                if kind == "qk":
                    ct, qk, half = c % KC, i % 2, i // 2
                    pe.wait_ge(s_wqk, 32)
                    pe.wait_ge(s_xT, 16 * (c // KC + 1))
                    for k in range(KC):
                        ins = pe.matmul(misc[:], wqkv[:, qk, k, P * ct:P * (ct + 1)],
                                        xT[:, k, HALF * half:HALF * (half + 1)],
                                        start=k == 0, stop=k == KC - 1)
                elif kind == "v":
                    pe.wait_ge(s_wv, 16)
                    pe.wait_ge(s_xT, 16 * (c + 1))
                    for t in range(2):
                        for k in range(KC):
                            tok = P * (2 * i + t)
                            ins = pe.matmul(misc[:, DIM * t:DIM * (t + 1)], xT[:, k, tok:tok + P],
                                            wqkv[:, 2, k, :], start=k == 0, stop=k == KC - 1)
                elif kind == "norms":
                    pe.wait_ge(s_setup, 1)
                    pe.wait_ge(s_square, 4 * c + i + 1)
                    ins = pe.matmul(misc[:], blocks[:], square[:], start=True, stop=True)
                elif kind == "count":
                    pe.wait_ge(s_over, c + 1)
                    ins = pe.matmul(misc[0:1, 0:1], over[:], ones_col[:], start=True, stop=True)
                elif kind == "project":
                    pe.wait_ge(s_aT, 16 * GH * 2 * GROUPS * (c + 1))
                    pe.wait_ge(s_const, 16 * NCONST)
                    for t in range(2):
                        for k in range(KC):
                            tok = P * (2 * i + t)
                            ins = pe.matmul(misc[:, DIM * t:DIM * (t + 1)], aT[:, k, tok:tok + P],
                                            woT[:, k, :], start=k == 0, stop=k == KC - 1)
                elif kind == "turn":
                    pe.wait_ge(s_x1, c + 1)
                    for t in range(2):
                        for k in range(KC):
                            ins = pe.transpose(misc[:, P * (KC * t + k):P * (KC * t + k + 1)],
                                               res[:, 2 * i + t, P * k:P * (k + 1)], ident[:])
                elif kind == "router":
                    for t in range(2):
                        for k in range(KC):
                            ins = pe.matmul(misc[:, EXPERTS * t:EXPERTS * (t + 1)], x1T[:, t, k, :],
                                            wr[:, k, :], start=k == 0, stop=k == KC - 1)
                elif kind == "place":
                    pe.wait_ge(s_mask, c + 1)
                    pos = misc[:, 0:TB * EXPERTS].rearrange("p (t e) -> p t e", e=EXPERTS)
                    pe.matmul(pos, tri[:], mask[:], start=True, stop=False)
                    for t in range(TB - 1):
                        pe.matmul(pos[:, t + 1:TB, :], ones[:],
                                  mask[:, t:t + 1, :].to_broadcast((P, TB - 1 - t, EXPERTS)),
                                  start=False, stop=False)
                    ins = pe.matmul(pos, ones[:], before[:].unsqueeze(1).to_broadcast((P, TB, EXPERTS)),
                                    start=False, stop=True)
                ins.then_inc(s_full, 1)

            def general_maxima(grp, jobs_before):
                par = grp % 2
                pe.wait_ge(s_flag, grp // 2 + 1)
                flag = pe.value_load(flags[0:1, grp // 2:grp // 2 + 1], min_val=0, max_val=P)
                with pe.If(flag > 0):
                    pe.wait_ge(s_free, jobs_before)
                    base = (GEN + 2) * grp
                    for j in range(GH):
                        for t in range(TB):
                            for half in range(2):
                                m = (j * TB + t) * 2 + half
                                if base + m:
                                    pe.wait_ge(g_free, base + m)
                                pe.matmul(misc[:], qst[par][0:ROWS, j, P * t:P * (t + 1)],
                                          kst[par][0:ROWS, j, HALF * half:HALF * (half + 1)],
                                          start=True, stop=True).then_inc(g_full, 1)
                    pe.wait_ge(g_free, base + GEN + 1)
                    pe.transpose(misc[0:GH * TB, 0:P], gneg[:], ident[:]).then_inc(g_full, 1)
                    pe.wait_ge(g_row, 16 * (grp + 1))
                with pe.Else():
                    pe.sem_inc(g_full, GEN + 1)

            def scores(s):
                grp, qh, kt = s // STEPS, s // TB % 2, s % TB
                par = grp % 2
                for pair in range(2):
                    u = 2 * s + pair
                    if u >= NSB:
                        pe.wait_ge(s_exp, u - NSB + 1)
                    for e in range(2):
                        j = 2 * pair + e
                        ins = pe.matmul(spsum[u % NSB][:, e, :], kst[par][:, j, P * kt:P * (kt + 1)],
                                        qst[par][:, j, HALF * qh:HALF * (qh + 1)], start=True, stop=True)
                    ins.then_inc(s_score, 1)

            def values(s):
                grp, kt = s // STEPS, s % TB
                b, h0 = grp // GROUPS, GH * (grp % GROUPS)
                pe.wait_ge(s_exp, 2 * s + 2)
                if kt == 0 and s >= TB:
                    pe.wait_ge(s_ofree, s // TB)
                for j in range(GH):
                    ins = pe.matmul(opsum[32 * j:32 * j + HD + 1, :], val[b % 2][:, kt, h0 + j, :],
                                    prob[(2 * s + j // 2) % NPB][:, HALF * (j % 2):HALF * (j % 2 + 1)],
                                    start=kt == 0, stop=kt == TB - 1)
                ins.then_inc(s_pv, 1)

            ran = 0
            for s in range(first, last + 1):
                if 0 <= s < NSTEP:
                    if s % STEPS == 0:
                        grp = s // STEPS
                        pe.wait_ge(s_fill[grp % 2], 112 * (grp // 2 + 1))
                        general_maxima(grp, ran)
                    scores(s)
                for job in jobs_at(s):
                    run(job)
                    ran += 1
                if 0 < s <= NSTEP:
                    if (s - 1) % (STEPS * GROUPS) == 0:
                        b = (s - 1) // (STEPS * GROUPS)
                        pe.wait_ge(s_free, number["v", b, 3] + 1)
                    values(s - 1)

        @block.vector
        def _(dve):
            links = [0]

            def link(ins):
                links[0] += 1
                ins.then_inc(s_chain, 1)
                dve.wait_ge(s_chain, links[0])

            counts = {}

            def tell(ins, s):
                counts[s.name] = counts.get(s.name, 0) + 1
                ins.then_inc(s, 1)
                dve.wait_ge(s, counts[s.name])

            link(dve.memset(ones_col[:], 1.0))
            link(dve.memset(opsum[:], 0.0))
            for i in range(2):
                link(dve.memset(kst[i][ROWS:ROWS + 1].bitcast(F32), 1.0))
            dve.wait_ge(s_trig, 32)
            link(dve.tensor_scalar(ang[:, 1, :], ang[:, 0, :], -2 * PI, 0.0, ALU.max, ALU.min))
            link(dve.tensor_scalar(ang[:, 1, :], ang[:, 1, :], PI, None, ALU.add))
            link(dve.scalar_tensor_tensor(ang[:, 2, :], ang[:, 1, :], -1.0, ang[:, 1, :], ALU.mult, ALU.min))
            tell(dve.tensor_scalar(ang[:, 2, :], ang[:, 2, :], PI / 2, None, ALU.add), s_angle)
            dve.wait_ge(s_sin, 1)
            link(dve.tensor_scalar(ang[:, 5, :], ang[:, 3, :], -1.0, None, ALU.mult))
            link(dve.tensor_scalar(ang[:, 4, :], ang[:, 4, :], -1.0, None, ALU.mult))

            def key_angles(ct):
                cosb, sinb, nsinb = ang[:, 4, ct:ct + 1], ang[:, 5, ct:ct + 1], ang[:, 3, ct:ct + 1]
                link(dve.tensor_scalar(ktrig[:, ct, 0, :], qtrig[:, 1, :], nsinb, None, ALU.mult))
                link(dve.scalar_tensor_tensor(ktrig[:, ct, 0, :], qtrig[:, 0, :], cosb,
                                              ktrig[:, ct, 0, :], ALU.mult, ALU.add))
                link(dve.tensor_scalar(ktrig[:, ct, 1, :], qtrig[:, 0, :], sinb, None, ALU.mult))
                link(dve.scalar_tensor_tensor(ktrig[:, ct, 1, :], qtrig[:, 1, :], cosb,
                                              ktrig[:, ct, 1, :], ALU.mult, ALU.add))

            def set_up():
                for i in range(2):
                    link(dve.memset(val[i][:, :, :, HD:HD + 1], 1.0))
                link(dve.memset(ones[:], 1.0))
                link(dve.memset(before[:], 0.0))
                dve.wait_ge(s_const, 16 * NCONST)
                link(dve.tensor_copy(tri[:], tri_f[:]))
                tell(dve.tensor_copy(blocks[:], blocks_f[:]), s_setup)

            def split_unit(c, i):
                ct, qk, half = c % KC, i % 2, i // 2
                u = 4 * c + i
                dve.wait_ge(s_soft, u + 1)
                tell(dve.scalar_tensor_tensor(raw[:], raw[:], 0.0, soft[:], ALU.max, ALU.add), s_raw)
                table = qtrig if qk == 0 else ktrig[:, ct]
                if u:
                    dve.wait_ge(s_split, u)
                link(dve.tensor_tensor(emb[:], raw[:].unsqueeze(1).to_broadcast((P, 2, HALF)),
                                       table[:, :, HALF * half:HALF * (half + 1)], ALU.mult))
                if u >= 2:
                    v = u - 2
                    dve.wait_ge(s_store[v % 4], 32 * (v // 4 + 1))
                tell(dve.tensor_copy(split[u % 2][:, 0], emb[:]), s_hi)

            def read_out(job):
                kind, c, i = (*job, 0)[:3]
                dve.wait_ge(s_full, number[job] + 1)
                if kind == "qk":
                    if u := 4 * c + i:
                        dve.wait_ge(s_square, u)
                    tell(dve.tensor_copy(raw[:], misc[:]), s_free)
                    tell(dve.scalar_tensor_tensor(soft[:], raw[:], -1.0, raw[:], ALU.mult, ALU.min), s_abs)
                elif kind == "v":
                    tell(dve.tensor_copy(val[c % 2][:, 2 * i:2 * i + 2, :, 0:HD],
                                         misc[:].rearrange("p (t h d) -> p t h d", t=2, h=HEADS)), s_free)
                elif kind == "norms":
                    qk, half = i % 2, i // 2
                    tell(dve.tensor_reduce(tops[:, 2 * qk + half:2 * qk + half + 1], misc[:], AX.X,
                                           ALU.max), s_free)
                    if i == 3:
                        for m in range(2):
                            link(dve.tensor_tensor(top2[:, m:m + 1], tops[:, 2 * m:2 * m + 1],
                                                   tops[:, 2 * m + 1:2 * m + 2], ALU.max))
                        link(dve.tensor_tensor(top2[:, 2:3], top2[:, 0:1], top2[:, 1:2], ALU.mult))
                        tell(dve.tensor_scalar(over[:], top2[:, 2:3], BOUND ** 2 * HD, None, ALU.is_gt),
                             s_over)
                elif kind == "count":
                    tell(dve.tensor_copy(flags[0:1, c:c + 1], misc[0:1, 0:1]), s_free)
                    tell_flag()
                elif kind == "project":
                    if i == 0:
                        dve.wait_ge(s_res, 16 * (c + 1))
                    r = res[:, 2 * i:2 * i + 2, 0:DIM]
                    tell(dve.tensor_tensor(r, misc[:].rearrange("p (t d) -> p t d", t=2), r, ALU.add),
                         s_free)
                    for t in (2 * i, 2 * i + 1):
                        link(dve.bn_stats(stats[:, t, :], res[:, t, 0:DIM]))
                        link(dve.bn_aggr(mv[:, t, :], stats[:, t, :]))
                    if i == 3:
                        tell(dve.tensor_scalar(lnt[:, 0, :], mv[:, :, 1], EPS, None, ALU.add), s_var)
                elif kind == "turn":
                    tell(dve.tensor_copy(x1T[:].rearrange("p t k n -> p (t k n)"), misc[:]), s_free)
                elif kind == "router":
                    tell(dve.tensor_tensor(
                        rt[:, 0, 2 * i:2 * i + 2, :],
                        misc[:, 0:2 * EXPERTS].rearrange("p (t e) -> p t e", e=EXPERTS),
                        br[:].unsqueeze(1).to_broadcast((P, 2, EXPERTS)), ALU.add), s_free)
                    if i == 3:
                        link(dve.tensor_reduce(rs[:, 0, :], rt[:, 0], AX.X, ALU.max))
                        tell(dve.tensor_tensor(rt[:, 1], rt[:, 0], wide(rs[:, 0, :]), ALU.subtract),
                             s_logit)
                elif kind == "place":
                    tell(dve.tensor_copy(rt[:, 6].rearrange("p t e -> p (t e)"),
                                         misc[:, 0:TB * EXPERTS]), s_free)
                    slots(c)

            def tell_flag():
                tell(dve.memset(top2[:, 0:1], 0.0), s_flag)

            def wide(a):
                return a.unsqueeze(2).to_broadcast((P, TB, EXPERTS))

            def norm(b):
                dve.wait_ge(s_rstd, b + 1)
                newton(dve, link, lnt)
                for t in range(TB):
                    ins = dve.tensor_scalar(res[:, t, 0:DIM], res[:, t, 0:DIM], mv[:, t, 0:1], lnt[:, 4, t:t + 1],
                                            ALU.subtract, ALU.mult)
                    if t < TB - 1:
                        link(ins)
                tell(ins, s_x1)

            def top_two(b):
                dve.wait_ge(s_gexp, b + 1)
                link(dve.tensor_reduce(rs[:, 1, :], rt[:, 1], AX.X, ALU.add))
                link(dve.reciprocal(rs[:, 2, :], rs[:, 1, :]))
                link(dve.tensor_tensor(rt[:, 2], rt[:, 1], wide(rs[:, 2, :]), ALU.mult))
                link(dve.tensor_copy(res[:, :, GATES:GATES + EXPERTS], rt[:, 2]))
                link(dve.tensor_copy(res[:, :, TOKEN], token_no[:, TB * b:TB * (b + 1)]))
                for k in range(2):
                    g, pick = rt[:, 2 + k], rt[:, 4 + k]
                    link(dve.tensor_reduce(rs[:, 3 + k, :], g, AX.X, ALU.max))
                    link(dve.tensor_tensor(rt[:, 7], g, wide(rs[:, 3 + k, :]), ALU.is_equal))
                    link(dve.tensor_tensor(rt[:, 7], rt[:, 7], rev[:], ALU.mult))
                    link(dve.tensor_reduce(rs[:, 5, :], rt[:, 7], AX.X, ALU.max))
                    link(dve.tensor_tensor(pick, rt[:, 7], wide(rs[:, 5, :]), ALU.is_equal))
                    if k == 0:
                        link(dve.scalar_tensor_tensor(rt[:, 3].rearrange("p t e -> p (t e)"),
                                                      pick.rearrange("p t e -> p (t e)"), -4.0,
                                                      g.rearrange("p t e -> p (t e)"),
                                                      ALU.mult, ALU.add))
                tell(dve.tensor_tensor(mask[:], rt[:, 4], rt[:, 5], ALU.add), s_mask)

            def slots(b):
                with nc.allow_low_precision(reason="counts of tiles, below 256: exact"):
                    link(dve.tensor_reduce(rs[:, 6, :], mask[:].rearrange("p t e -> p e t"), AX.X, ALU.add))
                    link(dve.tensor_tensor(before[:], before[:], rs[:, 6, :], ALU.add))
                link(dve.tensor_scalar(rt[:, 8], rt[:, 6], float(CAP), None, ALU.is_le))
                link(dve.tensor_tensor(rt[:, 9], rt[:, 6], slot_base[:], ALU.add))
                for k in range(2):
                    link(dve.tensor_tensor(rt[:, 10], rt[:, 4 + k], rt[:, 8], ALU.mult))
                    link(dve.tensor_reduce(rs[:, 7, :], rt[:, 10], AX.X, ALU.add))
                    link(dve.tensor_tensor(rt[:, 11], rt[:, 10], rt[:, 9], ALU.mult))
                    link(dve.tensor_reduce(rs[:, 8, :], rt[:, 11], AX.X, ALU.add))
                    link(dve.tensor_scalar(rs[:, 9, :], rs[:, 7, :], -float(OOB), float(OOB),
                                           ALU.mult, ALU.add))
                    if k == 0:
                        if b:
                            dve.wait_ge(s_scat, 16 * 2 * TB * b)
                    ins = dve.tensor_tensor(scatter_idx[:, k, :], rs[:, 8, :], rs[:, 9, :], ALU.add)
                    if k == 0:
                        link(ins)
                tell(ins, s_idx)

            def read_outputs(blk):
                dve.wait_ge(s_pv, TB * (blk + 1))
                if blk:
                    dve.wait_ge(s_norm, blk)
                tell(dve.tensor_copy(oraw[:], opsum[:]), s_ofree)

            def sums(blk):
                link(dve.stream_shuffle(oden[:], oraw[:], [HD] * 32))
                tell(dve.reciprocal(oden[:], oden[:]), s_sums)

            def general_maxima(grp):
                dve.wait_ge(s_flag, grp // 2 + 1)
                flag = dve.value_load(flags[0:1, grp // 2:grp // 2 + 1], min_val=0, max_val=P)
                with dve.If(flag > 0):
                    full, free = (GEN + 1) * grp, (GEN + 2) * grp
                    for m in range(GEN):
                        dve.wait_ge(g_full, full + m + 1)
                        dve.tensor_reduce(gmax[:, m:m + 1], misc[:], AX.X, ALU.max).then_inc(g_free, 1)
                    dve.wait_ge(g_free, free + GEN)
                    dve.tensor_reduce(gneg[:], gmax[:].rearrange("p (m h) -> p m h", h=2), AX.X, ALU.max,
                                      negate=True).then_inc(g_free, 1)
                    dve.wait_ge(g_full, full + GEN + 1)
                    dve.tensor_copy(grow[:], misc[0:GH * TB, 0:P]).then_inc(g_free, 1)
                    dve.wait_ge(g_free, free + GEN + 2)
                with dve.Else():
                    dve.sem_inc(g_free, GEN + 2)

            key_angles(0)
            for s in range(first, last + 1):
                if 0 < s <= NSTEP and s % TB == 0:
                    read_outputs(s // TB - 1)
                if 0 <= s < NSTEP and s % STEPS == 0:
                    general_maxima(s // STEPS)
                for job in jobs_at(s):
                    read_out(job)
                for job in jobs_at(s - 2):
                    if job[0] == "qk":
                        split_unit(*job[1:])
                if s == first + 2:
                    set_up()
                    key_angles(1)
                if (b := tail_at(s, "norm")) is not None:
                    norm(b)
                if (b := tail_at(s, "top")) is not None:
                    top_two(b)
                if TB <= s - 2 <= NSTEP and (s - 2) % TB == 0:
                    sums((s - 2) // TB - 1)


def newton(dve, link, lnt):
    link(dve.tensor_tensor(lnt[:, 3, :], lnt[:, 2, :], lnt[:, 2, :], ALU.mult))
    link(dve.tensor_tensor(lnt[:, 3, :], lnt[:, 3, :], lnt[:, 0, :], ALU.mult))
    link(dve.tensor_scalar(lnt[:, 3, :], lnt[:, 3, :], -0.5, 1.5, ALU.mult, ALU.add))
    link(dve.tensor_tensor(lnt[:, 4, :], lnt[:, 2, :], lnt[:, 3, :], ALU.mult))


def experts(nc, w1_d, b1_d, w2_d, b2_d, tile_d, disp_d, sum_d, ident, areas, out):
    TERMS = ((0, 0), (0, 1), (1, 0))
    with ExitStack() as ctx:
        sb = lambda name, shape, dt=F32: ctx.enter_context(nc.sbuf_tensor(name, shape, dt))
        sem = lambda name: ctx.enter_context(nc.semaphore(name))
        raw1, raw2, w1s_0, w2s_0 = weight_views(areas)
        w1s = [w1s_0, sb("w1s", [P, 2, KC, HIDDEN], F32R)[:]]
        w2s = [w2s_0, sb("w2s", [P, 2, HK, DIM], F32R)[:]]
        b1 = sb("b1", [P, EXPERTS, HK])
        b2 = sb("b2", [P, EXPERTS, DIM])
        tile_no = sb("tile_no", [P, ST])
        rows = [sb(f"rows{i}", [P, ST, WIDE]) for i in range(2)]
        extra = sb("extra", [P, ST])
        add_idx = [sb(f"add_idx{i}", [P, ST], I32) for i in range(2)]
        xe = [sb(f"xe{i}", [P, 2, KC, CAP], F32R) for i in range(2)]
        NH = 3
        hraw = [sb(f"hraw{i}", [P, CAP]) for i in range(NH)]
        hid = sb("hid", [P, 2 * HK * CAP], F32R)
        hids = hid[:].rearrange("p (s k n) -> p s k n", s=2, k=HK)
        biased = [sb(f"biased{i}", [P, DIM]) for i in range(2)]
        eo = [sb(f"eo{i}", [P, ST, DIM]) for i in range(2)]
        area_k = areas[0]
        half = KC * SEQ
        y = [area_k[:, half * i:half * (i + 1)].rearrange("p (t d) -> p t d", t=TB) for i in range(2)]
        y += [sb(f"y{i}", [P, TB, DIM])[:] for i in range(2, BATCH)]
        stats = sb("stats2", [P, TB, 6])
        mv = sb("mv2", [P, BATCH, TB, 2])
        lnt = sb("lnt2", [P, 6, TB])
        scale = sb("scale2", [P, BATCH, TB])
        shift = sb("shift2", [P, BATCH, TB])
        hp = [ctx.enter_context(nc.psum_tensor(f"hp{i}", [P, 2, HALF], F32)) for i in range(2)]
        yp = [ctx.enter_context(nc.psum_tensor(f"yp{i}", [P, HALF], F32)) for i in range(2)]
        tp = [ctx.enter_context(nc.psum_tensor(f"tp{i}", [P, HALF], F32)) for i in range(2)]

        s_bias, s_w = sem("s_bias"), sem("s_w")
        s_whi, s_wlo = sem("s_whi2"), sem("s_wlo2")
        s_rows = [sem(f"s_rows{i}") for i in range(2)]
        s_turn, s_xhi, s_turned = sem("s_turn"), sem("s_xhi"), sem("s_turned")
        s_h, s_gelu, s_hhi, s_hid = sem("s_h"), sem("s_gelu"), sem("s_hhi"), sem("s_hid")
        s_y, s_biased, s_eo, s_add = sem("s_y"), sem("s_biased"), sem("s_eo"), sem("s_add")
        s_index = sem("s_index")
        s_load = [sem(f"s_load{b}") for b in range(BATCH)]
        s_var, s_rstd = sem("s_var2"), sem("s_rstd2")
        s_scale, s_done, s_donea, s_out = sem("s_scale"), sem("s_done"), sem("s_done_act"), sem("s_out")
        s_chain, s_actchain = sem("s_chain2"), sem("s_actchain2")
        block = ctx.enter_context(nc.Block())

        TURNS = ((0, 1), (2,), (3,), (4,), ())

        @block.sync
        def _(sp):
            def load_rows(e):
                if e >= 2:
                    sp.wait_ge(s_eo, ST * (e - 1))
                sp.dma_start(rows[e % 2][:], disp_d[e * CAP:(e + 1) * CAP].rearrange("(t p) d -> p t d", p=P)
                             ).then_inc(s_rows[e % 2], 16)

            def load_weights(e):
                if e >= 2:
                    sp.wait_ge(s_wlo, 2 * (e - 1))
                sp.dma_start(raw1, w1_d[e].rearrange("(k p) n -> p k n", p=P)).then_inc(s_w, 16)
                sp.dma_start(raw2, w2_d[e].rearrange("(k p) n -> p k n", p=P)).then_inc(s_w, 16)

            load_rows(0)
            sp.dma_start(b1[:], b1_d).then_inc(s_bias, 16)
            sp.dma_start(tile_no[:], tile_d).then_inc(s_bias, 16)
            load_weights(1)
            load_rows(1)
            sp.dma_start(b2[:].rearrange("p e d -> p (e d)"), b2_d.to_broadcast((P, EXPERTS * DIM))
                         ).then_inc(s_bias, 16)
            for e in range(2, EXPERTS):
                load_weights(e)
                load_rows(e)
            sp.wait_ge(s_add, 16 * ST * EXPERTS)
            for b in range(BATCH):
                sp.dma_start(y[b], sum_d[b * SEQ:(b + 1) * SEQ].rearrange("(t p) d -> p t d", p=P)
                             ).then_inc(s_load[b], 16)
            for b in range(BATCH):
                sp.wait_ge(s_done, b + 1)
                sp.wait_ge(s_donea, b + 1)
                sp.dma_start(out[b].rearrange("(t p) d -> p t d", p=P), y[b]).then_inc(s_out, 16)
            sp.wait_ge(s_out, 16 * BATCH)

        @block.gpsimd
        def _(pool):
            def weight_remainders(e):
                for n, (raw_w, parts_w) in enumerate(((raw1, w1s[e % 2]), (raw2, w2s[e % 2]))):
                    pool.wait_ge(s_whi, 2 * (e - 1) + n + 1)
                    pool.tensor_tensor(parts_w[:, 1], raw_w, parts_w[:, 0].bitcast(F32),
                                       ALU.subtract).then_inc(s_wlo, 1)

            for e in range(EXPERTS):
                if e + 1 < EXPERTS:
                    weight_remainders(e + 1)
                pool.wait_ge(s_index, e + 1)
                if e:
                    pool.wait_ge(s_add, 16 * ST * e)
                for t in range(ST):
                    pool.wait_ge(s_eo, ST * e + t + 1)
                    pool.indirect_dma_start(
                        sum_d, bass.IndirectOffsetOnAxis(ap=add_idx[e % 2][:, t:t + 1], axis=0),
                        eo[e % 2][:, t, :], None, bounds_check=TOKENS + CAP - 1,
                        compute_op=ALU.add).then_inc(s_add, 16)

        @block.tensor
        def _(pe):
            def turn(e, t):
                n = ST * e + t
                pe.wait_ge(s_rows[e % 2], 16 * (e // 2 + 1))
                if n >= 2:
                    pe.wait_ge(s_turned, n - 1)
                for k in range(KC):
                    ins = pe.transpose(tp[n % 2][:, P * k:P * (k + 1)],
                                       rows[e % 2][:, t, P * k:P * (k + 1)], ident[:])
                ins.then_inc(s_turn, 1)

            for t in range(ST):
                turn(0, t)
            for e in range(EXPERTS):
                if e:
                    pe.wait_ge(s_wlo, 2 * e)
                pe.wait_ge(s_turned, ST * (e + 1))
                for m in range(HK):
                    n = HK * e + m
                    if n >= 2:
                        pe.wait_ge(s_gelu, n - 1)
                    for k in range(KC):
                        for i, (a, b) in enumerate(TERMS):
                            for h in range(2):
                                ins = pe.matmul(hp[n % 2][:, h, 0:CH],
                                                w1s[e % 2][:, b, k, P * m:P * (m + 1)],
                                                xe[e % 2][:, a, k, CH * h:CH * (h + 1)],
                                                start=k == 0 and i == 0, stop=k == KC - 1 and i == 2)
                    ins.then_inc(s_h, 1)
                for t in range(ST):
                    if e + 1 < EXPERTS:
                        for tt in TURNS[t]:
                            turn(e + 1, tt)
                    n = ST * e + t
                    if n >= 2:
                        pe.wait_ge(s_biased, n - 1)
                    for m in range(HK):
                        if t == 0:
                            pe.wait_ge(s_hid, HK * e + m + 1)
                        for i, (a, b) in enumerate(TERMS):
                            ins = pe.matmul(yp[n % 2][:, 0:DIM], hids[:, a, m, P * t:P * (t + 1)],
                                            w2s[e % 2][:, b, m, :], start=m == 0 and i == 0,
                                            stop=m == HK - 1 and i == 2)
                    ins.then_inc(s_y, 1)

        @block.scalar
        def _(act):
            def weight_half(e, n):
                raw_w, parts_w = ((raw1, w1s[e % 2]), (raw2, w2s[e % 2]))[n]
                act.wait_ge(s_w, 32 * e)
                if e >= 2:
                    act.wait_ge(s_y, ST * (e - 1))
                act.copy(parts_w[:, 0], raw_w).then_inc(s_whi, 1)

            act.wait_ge(s_bias, 48)
            for e in range(EXPERTS):
                for m in range(HK):
                    n = HK * e + m
                    act.wait_ge(s_h, n + 1)
                    if n >= NH:
                        act.wait_ge(s_hid, n - NH + 1)
                    act.activation(hraw[n % NH][:].rearrange("p (h n) -> p h n", h=2), hp[n % 2][:, :, 0:CH],
                                   ACT.Gelu, bias=b1[:, e, m:m + 1]).then_inc(s_gelu, 1)
                    if e + 1 < EXPERTS and m in (2, 4):
                        weight_half(e + 1, m // 2 - 1)
                for t in range(ST):
                    act.wait_ge(s_biased, ST * e + t + 1)
                    if t == 0 and e >= 2:
                        act.wait_ge(s_add, 16 * ST * (e - 1))
                    act.mul(eo[e % 2][:, t, :], biased[(ST * e + t) % 2][:],
                            rows[e % 2][:, t, GATES + e:GATES + e + 1]).then_inc(s_eo, 1)
            act.preload_act_table_set("natural_log_exp_and_others")

            def normalise(b):
                act.wait_ge(s_scale, b + 1)
                for t in range(TB // 2, TB):
                    ins = act.activation(y[b][:, t, :], y[b][:, t, :], ACT.Identity,
                                         bias=shift[:, b, t:t + 1], scale=scale[:, b, t:t + 1])
                ins.then_inc(s_donea, 1)

            for b in range(BATCH):
                act.wait_ge(s_var, b + 1)
                act.activation(lnt[:, 1, :], lnt[:, 0, :], ACT.Ln).then_inc(s_actchain, 1)
                act.wait_ge(s_actchain, b + 1)
                act.activation(lnt[:, 2, :], lnt[:, 1, :], ACT.Exp, scale=-0.5).then_inc(s_rstd, 1)
                normalise(b)

        @block.vector
        def _(dve):
            links = [0]

            def link(ins):
                links[0] += 1
                ins.then_inc(s_chain, 1)
                dve.wait_ge(s_chain, links[0])

            def turned(e, t):
                n = ST * e + t
                if t == 0 and e >= 2:
                    dve.wait_ge(s_h, HK * (e - 1))
                dve.wait_ge(s_turn, n + 1)
                src = tp[n % 2][:, 0:DIM].rearrange("p (k n) -> p k n", k=KC)
                hi, lo = (xe[e % 2][:, i, :, P * t:P * (t + 1)] for i in range(2))
                dve.tensor_copy(hi, src).then_inc(s_xhi, 1)
                dve.wait_ge(s_xhi, n + 1)
                dve.tensor_tensor(lo, src, hi.bitcast(F32), ALU.subtract).then_inc(s_turned, 1)

            def index(e):
                dve.wait_ge(s_rows[e % 2], 16 * (e // 2 + 1))
                token = rows[e % 2][:, :, TOKEN]
                if e >= 2:
                    dve.wait_ge(s_add, 16 * ST * (e - 1))
                link(dve.scalar_tensor_tensor(extra[:], token, float(TOKENS), tile_no[:], ALU.is_ge, ALU.mult))
                dve.tensor_tensor(add_idx[e % 2][:], extra[:], token, ALU.add).then_inc(s_index, 1)
                dve.wait_ge(s_index, e + 1)

            for t in range(ST):
                turned(0, t)
            dve.wait_ge(s_bias, 48)
            for e in range(EXPERTS):
                for m in range(HK):
                    n = HK * e + m
                    dve.wait_ge(s_gelu, n + 1)
                    if m == 0 and e:
                        dve.wait_ge(s_y, ST * e)
                    dve.tensor_copy(hids[:, 0, m], hraw[n % NH][:]).then_inc(s_hhi, 1)
                    dve.wait_ge(s_hhi, n + 1)
                    dve.tensor_tensor(hids[:, 1, m], hraw[n % NH][:], hids[:, 0, m].bitcast(F32),
                                      ALU.subtract).then_inc(s_hid, 1)
                    if m == 1:
                        index(e)
                for t in range(ST):
                    if e + 1 < EXPERTS:
                        for tt in TURNS[t]:
                            turned(e + 1, tt)
                    n = ST * e + t
                    dve.wait_ge(s_y, n + 1)
                    if n >= 2:
                        dve.wait_ge(s_eo, n - 1)
                    dve.tensor_tensor(biased[n % 2][:], yp[n % 2][:, 0:DIM], b2[:, e, :], ALU.add
                                      ).then_inc(s_biased, 1)

            for b in range(BATCH):
                dve.wait_ge(s_load[b], 16)
                for t in range(TB):
                    link(dve.bn_stats(stats[:, t, :], y[b][:, t, :]))
                    link(dve.bn_aggr(mv[:, b, t, :], stats[:, t, :]))
                dve.tensor_scalar(lnt[:, 0, :], mv[:, b, :, 1], EPS, None, ALU.add).then_inc(s_var, 1)
                dve.wait_ge(s_var, b + 1)
                dve.wait_ge(s_rstd, b + 1)
                newton(dve, link, lnt)
                link(dve.tensor_copy(scale[:, b], lnt[:, 4, :]))
                dve.scalar_tensor_tensor(shift[:, b], mv[:, b, :, 0], -1.0, scale[:, b], ALU.mult, ALU.mult
                                         ).then_inc(s_scale, 1)
                dve.wait_ge(s_scale, b + 1)
                for t in range(TB // 2):
                    ins = dve.tensor_scalar(y[b][:, t, :], y[b][:, t, :], scale[:, b, t:t + 1],
                                            shift[:, b, t:t + 1], ALU.mult, ALU.add)
                    if t < TB // 2 - 1:
                        link(ins)
                ins.then_inc(s_done, 1)
                dve.wait_ge(s_done, b + 1)


def kernel(L0_attn_x, L0_attn_wq, L0_attn_wk, L0_attn_wv, L0_attn_wo, L0_attn_pope_bias,
           L0_ffn_router_w, L0_ffn_router_b, L0_ffn_w1, L0_ffn_b1, L0_ffn_w2, L0_ffn_b2):
    import numpy as np
    import concourse.bacc as bacc
    from concourse.bass_utils import run_bass_kernel_spmd

    def parts(a):
        a = np.asarray(a)
        return np.ascontiguousarray(a.reshape(-1, P, a.shape[1]).transpose(1, 0, 2))

    x = np.asarray(L0_attn_x)
    pos = np.arange(SEQ, dtype=np.float32)
    inv = (10000.0 ** -(np.arange(HD) / HD)).astype(np.float32)
    angle = (pos[None, :] * inv[:, None]).astype(np.float32).astype(np.float64)
    trig = np.stack([np.cos(angle), np.sin(angle)], axis=1).astype(np.float32)
    e = np.arange(EXPERTS, dtype=np.float32)
    arrays = {
        "x": np.ascontiguousarray(x.reshape(BATCH, TB, P, DIM).transpose(0, 2, 1, 3)),
        "xT": np.ascontiguousarray(x.reshape(BATCH, SEQ, KC, P).transpose(0, 3, 2, 1)),
        "wq": parts(np.asarray(L0_attn_wq).T),
        "wk": parts(np.asarray(L0_attn_wk).T),
        "wv": parts(np.asarray(L0_attn_wv).T),
        "wo": parts(np.asarray(L0_attn_wo).T),
        "bias": np.ascontiguousarray(np.asarray(L0_attn_pope_bias).reshape(KC, P).T),
        "wr": parts(L0_ffn_router_w),
        "br": np.asarray(L0_ffn_router_b).reshape(1, EXPERTS),
        "w1": np.ascontiguousarray(L0_ffn_w1),
        "b1": np.ascontiguousarray(np.asarray(L0_ffn_b1).reshape(EXPERTS, HK, P).transpose(2, 0, 1)),
        "w2": np.ascontiguousarray(L0_ffn_w2),
        "b2": np.ascontiguousarray(np.asarray(L0_ffn_b2).reshape(1, EXPERTS * DIM)),
        "trig": np.ascontiguousarray(np.tile(trig, (P // HD, 1, 1))),
        "ident": np.eye(P, dtype=np.float32),
        "tri": np.triu(np.ones((P, P), np.float32)),
        "blocks": np.kron(np.eye(P // HD, dtype=np.float32), np.ones((HD, HD), np.float32)),
        "rev": np.tile(EXPERTS - e, (P, TB)).astype(np.float32),
        "base": np.tile(e * CAP - 1, (P, TB)).astype(np.float32),
        "blank": np.pad(TOKENS + np.arange(P, dtype=np.float32)[:, None], ((0, 0), (TOKEN, 0))),
        "number": np.arange(TOKENS, dtype=np.float32).reshape(BATCH * TB, P).T.copy(),
        "tile": np.tile(P * np.arange(ST, dtype=np.float32), (P, 1)),
    }
    nc = bacc.Bacc("TRN2", target_bir_lowering=False, num_devices=1)
    args = [nc.dram_tensor(f"in_{n}", a.shape, mybir.dt.from_np(a.dtype), kind="ExternalInput").ap()
            for n, a in arrays.items()]
    out = nc.dram_tensor("out", (BATCH, SEQ, DIM), F32, kind="ExternalOutput").ap()
    build(nc, *args, out)
    r = run_bass_kernel_spmd(nc, [{f"in_{n}": a for n, a in arrays.items()}], core_ids=[0])
    return r.results[0]["out"]
```

```python
from contextlib import ExitStack

import concourse.bass as bass
from concourse import mybir

F32 = mybir.dt.float32
F32R = mybir.dt.float32r
BF16 = mybir.dt.bfloat16
I32 = mybir.dt.int32
ALU = mybir.AluOpType
ACT = mybir.ActivationFunctionType
AX = mybir.AxisListType

P = 128
BATCH, SEQ, DIM, HEADS = 4, 1024, 256, 16
HD = DIM // HEADS
EXPERTS, HIDDEN = 8, 1024
TOKENS = BATCH * SEQ
CAP = -(-TOKENS * 5 // (EXPERTS * 4))
SLOTS = EXPERTS * CAP
EPS = 1e-5
PI = 3.1415927410125732

KC = DIM // P
TB = SEQ // P
GH = 4
GROUPS = HEADS // GH
HALF = SEQ // 2
STEPS = 2 * TB
NG = BATCH * GROUPS
NSTEP = NG * STEPS
ROWS = 3 * 2 * HD
BOUND = 60.0
ST = CAP // P
HK = HIDDEN // P
CH = CAP // 2
GATES = DIM
TOKEN = DIM + EXPERTS
WIDE = TOKEN + 1
OOB = 2 * SLOTS


def misc_schedule():
    at = {}

    def put(s, job):
        at.setdefault(s, []).append(job)

    for i in range(4):
        put(-14 + 3 * i, ("qk", 0, i))
        put(-10 + 3 * i, ("norms", 0, i))
        put(-13 + 3 * i, ("v", 0, i))
    put(-1, ("count", 0))
    for grp in range(0, NG - 2, 2):
        c, s0 = grp // 2 + 1, STEPS * grp
        for i in range(4):
            put(s0 + (1, 5, 9, 13)[i], ("qk", c, i))
            put(s0 + (6, 10, 14, 18)[i], ("norms", c, i))
        put(s0 + 19, ("count", c))
        if grp % GROUPS == 2:
            for i in range(4):
                put(s0 + STEPS + (4, 7, 12, 15)[i], ("v", grp // GROUPS + 1, i))
    for u, (b, t0, t1) in enumerate(UNITS):
        s0, t, tiles = STEPS * GROUPS * (b + 1), TAIL[u], range(t0 // 2, t1 // 2)
        for n, i in enumerate(tiles):
            put(s0 + t["project"][n], ("project", u, i))
        for n, i in enumerate(tiles):
            put(s0 + t["turn"][n], ("turn", u, i))
        for n, i in enumerate(tiles):
            put(s0 + t["router"][n], ("router", u, i))
        put(s0 + t["place"], ("place", u))
    return at


UNITS = [(b, 0, TB) for b in range(BATCH - 1)] + [(BATCH - 1, 0, TB // 2), (BATCH - 1, TB // 2, TB)]
TAIL = [dict(project=(11, 12, 15, 16), rstd=17, norm=18, norm2=19, turn=(22, 24, 26, 27),
             router=(23, 25, 28, 29), exp=30, top=31, place=36)] * (BATCH - 1) + [
    dict(project=(-1, 0), rstd=1, norm=1, norm2=1, turn=(2, 3), router=(3, 4), exp=5, top=5,
         place=9),
    dict(project=(6, 7), rstd=7, norm=7, norm2=7, turn=(10, 11), router=(11, 12), exp=13, top=13,
         place=14)]


def build(nc, x_d, xT_d, wq_d, wk_d, wv_d, wo_d, bias_d, wr_d, br_d, w1_d, b1_d, w2_d, b2_d,
          trig_d, ident_d, tri_d, blocks_d, rev_d, base_d, blank_d, number_d, tile_d, out):
    jobs = misc_schedule()
    first, last = min(jobs), NSTEP + TAIL[-1]["place"] + 1
    number, n = {}, 0
    for s in range(first, last + 1):
        for job in jobs.get(s, ()):
            number[job] = n
            n += 1

    split_d = nc.dram_tensor("split_scratch", (2, BATCH, 2, HEADS, 2 * HD, SEQ), F32).ap()
    disp_d = nc.dram_tensor("dispatched", (SLOTS, WIDE), F32).ap()
    sum_d = nc.dram_tensor("sum_scratch", (TOKENS + CAP, DIM), F32).ap()

    with ExitStack() as both:
        sb2 = lambda name, shape, dt=F32: both.enter_context(nc.sbuf_tensor(name, shape, dt))
        ident = sb2("ident", [P, P])
        area_k = sb2("area_k", [P, KC * 2 * SEQ])
        area_q = sb2("area_q", [P, GH, SEQ], F32R)
        area_s = sb2("area_s", [P, 2 * 2 * 2 * HALF], F32R)
        areas = (area_k, area_q, area_s)
        attention(nc, jobs, number, first, last, x_d, xT_d, wq_d, wk_d, wv_d, wo_d, bias_d, wr_d,
                  br_d, trig_d, ident_d, tri_d, blocks_d, rev_d, base_d, blank_d, number_d, w1_d,
                  w2_d, split_d, disp_d, sum_d, ident, areas)
        experts(nc, w1_d, b1_d, w2_d, b2_d, tile_d, disp_d, sum_d, ident, areas, out)


def weight_views(areas):
    area_k, area_q, area_s = areas
    raw1 = area_k[:, 0:KC * HIDDEN].rearrange("p (k n) -> p k n", k=KC)
    raw2 = area_k[:, KC * HIDDEN:].rearrange("p (k n) -> p k n", k=HK)
    w1s = area_s[:].rearrange("p (s k n) -> p s k n", s=2, k=KC)
    w2s = area_q[:].rearrange("p (s a) n -> p s (a n)", s=2).rearrange("p s (k n) -> p s k n", k=HK)
    return raw1, raw2, w1s, w2s


def attention(nc, jobs, number, first, last, x_d, xT_d, wq_d, wk_d, wv_d, wo_d, bias_d, wr_d, br_d,
              trig_d, ident_d, tri_d, blocks_d, rev_d, base_d, blank_d, number_d, w1_d, w2_d,
              split_d, disp_d, sum_d, ident, areas):
    with ExitStack() as ctx:
        sb = lambda name, shape, dt=F32: ctx.enter_context(nc.sbuf_tensor(name, shape, dt))
        sem = lambda name: ctx.enter_context(nc.semaphore(name))

        area_k, area_q, area_s = areas
        qtrig = sb("qtrig", [P, 2, SEQ])[:]
        ktrig = area_k[:].rearrange("p (k t n) -> p k t n", k=KC, t=2)
        raw1, raw2, w1s, w2s = weight_views(areas)
        wqkv = sb("wqkv", [P, 3, KC, DIM])
        woT = sb("woT", [P, KC, DIM])
        wr = sb("wr", [P, KC, EXPERTS])
        br = sb("br", [P, EXPERTS])
        tri_f = sb("tri_f", [P, P])
        tri = sb("tri", [P, P], BF16)
        ones = sb("ones", [P, P], BF16)
        blocks_f = sb("blocks_f", [P, P])
        blocks = sb("blocks", [P, P], BF16)
        square = sb("square", [P, HALF], BF16)
        ones_col = sb("ones_col", [P, 1])
        rev = sb("rev", [P, TB, EXPERTS])
        slot_base = sb("slot_base", [P, TB, EXPERTS])
        blank = sb("blank", [P, WIDE])
        token_no = sb("token_no", [P, BATCH * TB])
        ang = sb("ang", [P, 6, KC])
        xT = sb("xT", [P, KC, SEQ])[:]
        raw = sb("raw", [P, HALF])
        soft = sb("soft", [P, HALF])
        emb = sb("emb", [P, 2, HALF])
        split = [area_s[:, 4 * HALF * i:4 * HALF * (i + 1)].rearrange("p (s t n) -> p s t n", s=2, t=2)
                 for i in range(2)]
        tops = sb("tops", [P, 4])
        top2 = sb("top2", [P, 3])
        over = sb("over", [P, 1])
        flags = sb("flags", [1, NG // 2], I32)
        qst = [area_q[0:ROWS + 1], sb("qst1", [ROWS + 1, GH, SEQ], F32R)[:]]
        kst = [sb(f"kst{i}", [ROWS + 1, GH, SEQ], F32R) for i in range(2)]
        val = [sb(f"val{i}", [P, TB, HEADS, HD + 1]) for i in range(2)]
        NPB, NSB = 4, 3
        prob = [sb(f"prob{i}", [P, 2 * HALF]) for i in range(NPB)]
        oraw = sb("oraw", [P, HALF])
        oden = sb("oden", [P, HALF])
        onorm = sb("onorm", [P, HALF])
        aT = sb("aT", [P, KC, SEQ])
        res = sb("res", [P, TB, WIDE])
        stats = sb("stats", [P, TB, 6])
        mv = sb("mv", [P, TB, 2])
        lnt = sb("lnt", [P, 5, TB])
        x1T = [sb(f"x1T{i}", [P, 2, KC, P]) for i in range(2)]
        rt = sb("rt", [P, 12, TB, EXPERTS])
        rs = sb("rs", [P, 16, TB])
        mask = sb("mask", [P, TB, EXPERTS], BF16)
        before = sb("before", [P, EXPERTS], BF16)
        scatter_idx = sb("scatter_idx", [P, 2, TB], I32)
        gmax = sb("gmax", [P, 2 * GH * TB])
        gneg = sb("gneg", [P, GH * TB])
        grow = sb("grow", [GH * TB, P], F32R)

        spsum = [ctx.enter_context(nc.psum_tensor(f"spsum{i}", [P, 2, HALF], F32)) for i in range(NSB)]
        opsum = ctx.enter_context(nc.psum_tensor("opsum", [P, HALF], F32))
        misc = ctx.enter_context(nc.psum_tensor("misc", [P, HALF], F32))

        s_bias, s_krow = sem("s_bias"), sem("s_krow")
        s_wqk, s_trig, s_wv = sem("s_wqk"), sem("s_trig"), sem("s_wv")
        s_setup, s_sums = sem("s_setup"), sem("s_sums")
        s_raw, s_hi = sem("s_raw"), sem("s_hi")
        s_const, s_xT, s_res, s_zero = sem("s_const"), sem("s_xT"), sem("s_res"), sem("s_zero")
        s_blank, s_w0, s_whi = sem("s_blank"), sem("s_w0"), sem("s_whi")
        s_chain = sem("s_chain")
        s_actchain = sem("s_actchain")
        s_angle, s_sin = sem("s_angle"), sem("s_sin")
        s_full, s_free = sem("s_misc_full"), sem("s_misc_free")
        s_abs, s_soft = sem("s_abs"), sem("s_soft")
        s_split = sem("s_split")
        s_half = sem("s_half")
        s_first = [sem(f"s_first{i}") for i in range(4)]
        s_store = [sem(f"s_store{i}") for i in range(4)]
        s_square, s_over, s_flag = sem("s_square"), sem("s_over"), sem("s_flag")
        s_fill = [sem(f"s_fill{i}") for i in range(2)]
        s_score, s_exp, s_pv = sem("s_score"), sem("s_exp"), sem("s_pv")
        s_ofree, s_norm, s_aT = sem("s_ofree"), sem("s_onorm"), sem("s_aT")
        s_var, s_rstd, s_x1 = sem("s_var"), sem("s_rstd"), sem("s_x1")
        s_logit, s_gexp, s_mask, s_idx = sem("s_logit"), sem("s_gexp"), sem("s_mask"), sem("s_idx")
        s_scat, s_x1d = sem("s_scat"), sem("s_x1d")
        g_full, g_free, g_row = sem("s_gen_full"), sem("s_gen_free"), sem("s_gen_row")
        GEN = 2 * GH * TB

        NCONST = 9
        block = ctx.enter_context(nc.Block())

        early = sum(len(jobs.get(s, ())) for s in range(first, 0))
        late = sum(len(jobs.get(s, ())) for s in range(first, NSTEP + 1))
        banks = [misc, *(b[:, 0, :] for b in spsum)]

        def bank(job):
            n = number[job]
            if n < early:
                return banks[n % len(banks)]
            return banks[(n - late) % len(banks)] if n >= late else misc

        def jobs_at(s):
            return jobs.get(s, ())

        def sums_at(s, part):
            if s == NSTEP:
                return 2 * NG - 1
            if s == NSTEP - TB + 1 + part:
                return 2 * NG - 2
            s -= (2, 6)[part]
            return s // TB - 1 if TB <= s < NSTEP - TB and s % TB == 0 else None

        def tail_at(s, what):
            for u, (b, _, _) in enumerate(UNITS):
                if s == STEPS * GROUPS * (b + 1) + TAIL[u][what]:
                    return u
            return None

        def filled(eng, grp):
            if grp == 0:
                eng.wait_ge(s_half, 112)
            eng.wait_ge(s_fill[grp % 2], 112 * (grp // 2 + 1) - 16 * (grp % 2 == 0))

        def stored(eng, c, i):
            if c:
                eng.wait_ge(s_store[i], 32 * c)
            else:
                eng.wait_ge(s_first[i], 32)

        def store(eng, c, i):
            b, ct, qk, half = c // KC, c % KC, i % 2, i // 2
            u = 4 * c + i
            eng.wait_ge(s_hi, u + 1)
            eng.wait_ge(s_split, u + 1)
            for part in range(2):
                eng.dma_start(split_d[qk, b, part, 8 * ct:8 * ct + 8, :, HALF * half:HALF * (half + 1)]
                              .rearrange("h (d t) n -> (h d) t n", t=2),
                              split[u % 2][:, part].bitcast(F32)
                              ).then_inc(s_store[i] if c else s_first[i], 16)

        @block.sync
        def _(sp):
            sp.dma_start(ang[:, 0, :], bias_d).then_inc(s_bias, 16)
            sp.dma_start(wqkv[:, 0], wq_d).then_inc(s_wqk, 16)
            sp.dma_start(xT, xT_d[0]).then_inc(s_xT, 16)
            sp.dma_start(wqkv[:, 1], wk_d).then_inc(s_wqk, 16)
            sp.dma_start(qtrig, trig_d).then_inc(s_trig, 16)
            sp.dma_start(blank[:], blank_d).then_inc(s_blank, 16)
            sp.dma_start(wqkv[:, 2], wv_d).then_inc(s_wv, 16)
            sp.dma_start(woT[:], wo_d).then_inc(s_const, 16)
            sp.dma_start(wr[:], wr_d).then_inc(s_const, 16)
            sp.dma_start(br[:], br_d.to_broadcast((P, EXPERTS))).then_inc(s_const, 16)
            sp.dma_start(ident[:], ident_d).then_inc(s_const, 16)
            sp.dma_start(tri_f[:], tri_d).then_inc(s_const, 16)
            sp.dma_start(blocks_f[:], blocks_d).then_inc(s_const, 16)
            sp.dma_start(rev[:].rearrange("p t e -> p (t e)"), rev_d).then_inc(s_const, 16)
            sp.dma_start(token_no[:], number_d).then_inc(s_const, 16)
            sp.dma_start(slot_base[:].rearrange("p t e -> p (t e)"), base_d).then_inc(s_const, 16)
            sp.dma_start(res[:, :, 0:DIM], x_d[0]).then_inc(s_res, 16)

            def fill_half(n):
                for i in (2 * n, 2 * n + 1):
                    stored(sp, 0, i)
                cols = slice(HALF * n, HALF * (n + 1))
                for qk, stack, terms in ((0, qst, (0, 0, 1)), (1, kst, (0, 1, 0))):
                    for r, part in enumerate(terms):
                        sp.dma_start(stack[0][2 * HD * r:2 * HD * (r + 1), :, cols].bitcast(F32),
                                     split_d[qk, 0, part, 0:GH, :, cols].rearrange("h r n -> r h n")
                                     ).then_inc(s_fill[0] if n else s_half, 16)

            def fill(grp):
                b, h0, par = grp // GROUPS, GH * (grp % GROUPS), grp % 2
                for i in range(4):
                    stored(sp, grp // 2, i)
                if grp >= 2:
                    sp.wait_ge(s_score, 2 * STEPS * (grp - 1))
                for qk, stack, terms in ((0, qst, (0, 0, 1)), (1, kst, (0, 1, 0))):
                    for r, part in enumerate(terms):
                        sp.dma_start(stack[par][2 * HD * r:2 * HD * (r + 1)].bitcast(F32),
                                     split_d[qk, b, part, h0:h0 + GH].rearrange("h r n -> r h n")
                                     ).then_inc(s_fill[par], 16)
                zero_row(grp, s_fill[par])
                add_maxima(grp)

            def zero_row(grp, done):
                sp.dma_start(qst[grp % 2][ROWS:ROWS + 1].bitcast(F32),
                             blank[0:GH * SEQ // DIM, 0:DIM]).then_inc(done, 16)

            def add_maxima(grp):
                par = grp % 2
                sp.wait_ge(s_flag, grp // 2 + 1)
                flag = sp.value_load(flags[0:1, grp // 2:grp // 2 + 1], min_val=0, max_val=P)
                with sp.If(flag > 0):
                    sp.wait_ge(g_free, (GEN + 2) * (grp + 1))
                    filled(sp, grp)
                    sp.dma_start(qst[par][ROWS:ROWS + 1].bitcast(F32),
                                 grow[:].bitcast(F32)).then_inc(g_row, 16)
                with sp.Else():
                    sp.sem_inc(g_row, 16)

            def gather_heads(blk):
                b, g, qh = blk // (2 * GROUPS), blk // 2 % GROUPS, blk % 2
                sp.wait_ge(s_norm, blk + 1)
                if b and blk % (2 * GROUPS) == 0:
                    sp.wait_ge(s_full, number["project", b - 1, 3] + 1)
                for j in range(GH):
                    r = (g % 2) * GH * HD + HD * j
                    sp.dma_start(aT[r:r + HD, g // 2, HALF * qh:HALF * (qh + 1)],
                                 onorm[32 * j:32 * j + HD, :]).then_inc(s_aT, 16)

            sp.wait_ge(s_blank, 16)
            zero_row(0, s_half)
            for n in range(2):
                store(sp, 0, 2 * n)
                store(sp, 0, 2 * n + 1)
                fill_half(n)
            add_maxima(0)
            fill(1)
            for grp in range(NG):
                b = grp // GROUPS
                if grp:
                    gather_heads(2 * grp - 1)
                if 1 <= grp < NG - 1:
                    fill(grp + 1)
                if grp % GROUPS == 1 and b < BATCH - 1:
                    sp.wait_ge(s_full, number["qk", 2 * b + 1, 3] + 1)
                    sp.dma_start(xT, xT_d[b + 1]).then_inc(s_xT, 16)
                if grp % GROUPS == 3 and b:
                    sp.wait_ge(s_scat, 16 * 2 * TB * b)
                    sp.wait_ge(s_x1d, 16 * b)
                    sp.dma_start(res[:, :, 0:DIM], x_d[b]).then_inc(s_res, 16)
                gather_heads(2 * grp)
                if grp == NG - 2:
                    sp.wait_ge(s_hi, NG * 2)
                    sp.dma_start(raw1, w1_d[0].rearrange("(k p) n -> p k n", p=P)).then_inc(s_w0, 16)
                    sp.dma_start(raw2, w2_d[0].rearrange("(k p) n -> p k n", p=P)).then_inc(s_w0, 16)
            gather_heads(2 * NG - 1)

        @block.gpsimd
        def _(pool):
            for i in range(2):
                pool.memset(kst[i][ROWS:ROWS + 1].bitcast(F32), 1.0).then_inc(s_krow, 1)
                pool.wait_ge(s_krow, i + 1)

            def clear_slots():
                pool.wait_ge(s_blank, 16)
                pool.dma_start(disp_d.rearrange("(t p) d -> p t d", p=P),
                               blank[:].unsqueeze(1).to_broadcast((P, SLOTS // P, WIDE))
                               ).then_inc(s_zero, 16)
                pool.dma_start(sum_d[TOKENS:].rearrange("(t p) d -> p t d", p=P),
                               blank[:, 0:DIM].unsqueeze(1).to_broadcast((P, ST, DIM))
                               ).then_inc(s_zero, 16)

            def split_rest(c, i):
                u = 4 * c + i
                pool.wait_ge(s_raw, u + 1)
                if u:
                    pool.wait_ge(s_full, number["norms", (u - 1) // 4, (u - 1) % 4] + 1)
                pool.tensor_tensor(square[:], raw[:], raw[:], ALU.mult).then_inc(s_square, 1)
                pool.wait_ge(s_hi, u + 1)
                pool.tensor_tensor(split[u % 2][:, 1], emb[:], split[u % 2][:, 0].bitcast(F32),
                                   ALU.subtract).then_inc(s_split, 1)
                if c:
                    store(pool, c, i)

            def save(u):
                b, t0, t1 = UNITS[u]
                pool.wait_ge(s_x1, u + 1)
                pool.dma_start(sum_d[b * SEQ + P * t0:b * SEQ + P * t1].rearrange("(t p) d -> p t d", p=P),
                               res[:, t0:t1, 0:DIM]).then_inc(s_x1d, 16)
                pool.wait_ge(s_idx, u + 1)
                pool.wait_ge(s_zero, 32)

            def scatter(u, tiles):
                for t in tiles:
                    for k in range(2):
                        pool.indirect_dma_start(
                            disp_d, bass.IndirectOffsetOnAxis(ap=scatter_idx[:, k, t:t + 1], axis=0),
                            res[:, t, :], None, bounds_check=SLOTS - 1,
                            oob_is_err=False).then_inc(s_scat, 16)

            def normalise(blk):
                pool.wait_ge(s_sums, 2 * blk + 2)
                if blk:
                    pool.wait_ge(s_aT, 16 * GH * blk)
                pool.tensor_tensor(onorm[:], oraw[:], oden[:], ALU.mult).then_inc(s_norm, 1)

            def weight_remainders():
                for n, (raw_w, parts_w) in enumerate(((raw1, w1s), (raw2, w2s))):
                    pool.wait_ge(s_whi, n + 1)
                    pool.tensor_tensor(parts_w[:, 1], raw_w, parts_w[:, 0].bitcast(F32), ALU.subtract)

            for s in range(first, last + 1):
                for job in jobs_at(s - 2):
                    if job[0] == "qk":
                        split_rest(*job[1:])
                if s == 4:
                    clear_slots()
                if s == NSTEP + 1:
                    weight_remainders()
                if (blk := sums_at(s, 1)) is not None:
                    normalise(blk)
                for u, (b, t0, t1) in enumerate(UNITS):
                    t = s - (STEPS * GROUPS * (b + 1) + TAIL[u]["place"])
                    if t == 0:
                        save(u)
                    if b < BATCH - 1 and t % 2 == 0 and t0 <= t // 2 < t1:
                        scatter(u, (t // 2,))
                    elif b == BATCH - 1 and t == 0:
                        scatter(u, range(t0, t1))
            pool.wait_ge(s_scat, 16 * 2 * TB * BATCH)
            pool.wait_ge(s_x1d, 16 * len(UNITS))

        @block.scalar
        def _(act):
            done = [0]

            def chained(ins):
                done[0] += 1
                ins.then_inc(s_actchain, 1)
                act.wait_ge(s_actchain, done[0])

            act.wait_ge(s_angle, 1)
            act.activation(ang[:, 3:5, :], ang[:, 1:3, :], ACT.Sin).then_inc(s_sin, 1)
            act.preload_act_table_set("natural_log_exp_and_others")

            def softplus(u):
                act.wait_ge(s_abs, u + 1)
                chained(act.activation(soft[:], soft[:], ACT.Exp))
                act.activation(soft[:], soft[:], ACT.Ln, bias=1.0).then_inc(s_soft, 1)

            def rstd_guess(u):
                _, t0, t1 = UNITS[u]
                act.wait_ge(s_var, u + 1)
                chained(act.activation(lnt[:, 1, t0:t1], lnt[:, 0, t0:t1], ACT.Ln))
                act.activation(lnt[:, 2, t0:t1], lnt[:, 1, t0:t1], ACT.Exp, scale=-0.5).then_inc(s_rstd, 1)

            def weight_halves():
                act.wait_ge(s_w0, 32)
                for i in range(4):
                    stored(act, NG // 2 - 1, i)
                act.copy(w1s[:, 0], raw1).then_inc(s_whi, 1)
                act.wait_ge(s_score, 2 * STEPS * (NG - 1))
                act.copy(w2s[:, 0], raw2).then_inc(s_whi, 1)

            def gates_exp(u):
                _, t0, t1 = UNITS[u]
                act.wait_ge(s_logit, u + 1)
                act.activation(rt[:, 1, t0:t1], rt[:, 1, t0:t1], ACT.Exp).then_inc(s_gexp, 1)

            for s in range(first, last + 1):
                if 0 <= s < NSTEP:
                    for u in (2 * s, 2 * s + 1):
                        act.wait_ge(s_score, u + 1)
                        if u >= NPB:
                            act.wait_ge(s_pv, (u - NPB) // 2 + 1)
                        act.activation(prob[u % NPB][:], spsum[u % NSB][:].rearrange("p a n -> p (a n)"),
                                       ACT.Exp, scale=HD ** -0.5).then_inc(s_exp, 1)
                for job in jobs_at(s - 1):
                    if job[0] == "qk":
                        softplus(4 * job[1] + job[2])
                if s == NSTEP:
                    weight_halves()
                if (u := tail_at(s, "rstd")) is not None:
                    rstd_guess(u)
                if (u := tail_at(s, "exp")) is not None:
                    gates_exp(u)

        @block.tensor
        def _(pe):
            def begin(job):
                n = number[job]
                if n >= late:
                    pe.wait_ge(s_free, max(n - len(banks) + 1, late))
                elif n >= early:
                    pe.wait_ge(s_free, n)
                elif n >= len(banks):
                    pe.wait_ge(s_free, n - len(banks) + 1)

            def run(job):
                kind, c, i = (*job, 0)[:3]
                misc = bank(job)
                begin(job)
                if kind == "qk":
                    ct, qk, half = c % KC, i % 2, i // 2
                    pe.wait_ge(s_wqk, 32)
                    pe.wait_ge(s_xT, 16 * (c // KC + 1))
                    for k in range(KC):
                        ins = pe.matmul(misc[:], wqkv[:, qk, k, P * ct:P * (ct + 1)],
                                        xT[:, k, HALF * half:HALF * (half + 1)],
                                        start=k == 0, stop=k == KC - 1)
                elif kind == "v":
                    pe.wait_ge(s_wv, 16)
                    pe.wait_ge(s_xT, 16 * (c + 1))
                    for t in range(2):
                        for k in range(KC):
                            tok = P * (2 * i + t)
                            ins = pe.matmul(misc[:, DIM * t:DIM * (t + 1)], xT[:, k, tok:tok + P],
                                            wqkv[:, 2, k, :], start=k == 0, stop=k == KC - 1)
                elif kind == "norms":
                    pe.wait_ge(s_setup, 1)
                    pe.wait_ge(s_square, 4 * c + i + 1)
                    ins = pe.matmul(misc[:], blocks[:], square[:], start=True, stop=True)
                elif kind == "count":
                    pe.wait_ge(s_over, c + 1)
                    ins = pe.matmul(misc[0:1, 0:1], over[:], ones_col[:], start=True, stop=True)
                elif kind == "project":
                    b, _, t1 = UNITS[c]
                    pe.wait_ge(s_aT, 16 * GH * (2 * GROUPS * (b + 1) - (t1 < TB)))
                    pe.wait_ge(s_const, 16 * NCONST)
                    for t in range(2):
                        for k in range(KC):
                            tok = P * (2 * i + t)
                            ins = pe.matmul(misc[:, DIM * t:DIM * (t + 1)], aT[:, k, tok:tok + P],
                                            woT[:, k, :], start=k == 0, stop=k == KC - 1)
                elif kind == "turn":
                    pe.wait_ge(s_x1, c + 1)
                    for t in range(2):
                        for k in range(KC):
                            ins = pe.transpose(misc[:, P * (KC * t + k):P * (KC * t + k + 1)],
                                               res[:, 2 * i + t, P * k:P * (k + 1)], ident[:])
                elif kind == "router":
                    pe.wait_ge(s_free, number["turn", c, i] + 1)
                    for t in range(2):
                        for k in range(KC):
                            ins = pe.matmul(misc[:, EXPERTS * t:EXPERTS * (t + 1)], x1T[i % 2][:, t, k, :],
                                            wr[:, k, :], start=k == 0, stop=k == KC - 1)
                elif kind == "place":
                    pe.wait_ge(s_mask, c + 1)
                    _, t0, t1 = UNITS[c]
                    pos = misc[:, 0:(t1 - t0) * EXPERTS].rearrange("p (t e) -> p t e", e=EXPERTS)
                    pe.matmul(pos, tri[:], mask[:, t0:t1], start=True, stop=False)
                    for t in range(t0, t1 - 1):
                        pe.matmul(pos[:, t - t0 + 1:, :], ones[:],
                                  mask[:, t:t + 1, :].to_broadcast((P, t1 - 1 - t, EXPERTS)),
                                  start=False, stop=False)
                    ins = pe.matmul(pos, ones[:],
                                    before[:].unsqueeze(1).to_broadcast((P, t1 - t0, EXPERTS)),
                                    start=False, stop=True)
                ins.then_inc(s_full, 1)

            def first_step(grp):
                par, s = grp % 2, STEPS * grp
                pe.wait_ge(s_flag, grp // 2 + 1)
                flag = pe.value_load(flags[0:1, grp // 2:grp // 2 + 1], min_val=0, max_val=P)
                with pe.If(flag > 0):
                    if grp:
                        values(s - 1)
                    pe.wait_ge(s_free, sum(len(jobs_at(i)) for i in range(first, s)))
                    filled(pe, grp)
                    base = (GEN + 2) * grp
                    for j in range(GH):
                        for t in range(TB):
                            for half in range(2):
                                m = (j * TB + t) * 2 + half
                                if base + m:
                                    pe.wait_ge(g_free, base + m)
                                pe.matmul(misc[:], qst[par][0:ROWS, j, P * t:P * (t + 1)],
                                          kst[par][0:ROWS, j, HALF * half:HALF * (half + 1)],
                                          start=True, stop=True).then_inc(g_full, 1)
                    pe.wait_ge(g_free, base + GEN + 1)
                    pe.transpose(misc[0:GH * TB, 0:P], gneg[:], ident[:]).then_inc(g_full, 1)
                    pe.wait_ge(g_row, 16 * (grp + 1))
                    scores(s)
                    for job in jobs_at(s):
                        run(job)
                with pe.Else():
                    pe.sem_inc(g_full, GEN + 1)
                    scores(s)
                    for job in jobs_at(s):
                        run(job)
                    if grp:
                        values(s - 1)

            def scores(s):
                grp, qh, kt = s // STEPS, s // TB % 2, s % TB
                par = grp % 2
                for pair in range(2):
                    u = 2 * s + pair
                    if u >= NSB:
                        pe.wait_ge(s_exp, u - NSB + 1)
                    for e in range(2):
                        j = 2 * pair + e
                        ins = pe.matmul(spsum[u % NSB][:, e, :], kst[par][:, j, P * kt:P * (kt + 1)],
                                        qst[par][:, j, HALF * qh:HALF * (qh + 1)], start=True, stop=True)
                    ins.then_inc(s_score, 1)

            def values(s):
                grp, kt = s // STEPS, s % TB
                b, h0 = grp // GROUPS, GH * (grp % GROUPS)
                if s % (STEPS * GROUPS) == 0:
                    pe.wait_ge(s_free, number["v", b, 3] + 1)
                pe.wait_ge(s_exp, 2 * s + 2)
                if kt == 0 and s >= TB:
                    pe.wait_ge(s_ofree, s // TB)
                for j in range(GH):
                    ins = pe.matmul(opsum[32 * j:32 * j + HD + 1, :], val[b % 2][:, kt, h0 + j, :],
                                    prob[(2 * s + j // 2) % NPB][:, HALF * (j % 2):HALF * (j % 2 + 1)],
                                    start=kt == 0, stop=kt == TB - 1)
                ins.then_inc(s_pv, 1)

            for s in range(first, last + 1):
                if s == 0:
                    pe.wait_ge(s_free, early)
                    pe.wait_ge(s_krow, 2)
                if 0 <= s < NSTEP and s % STEPS == 0:
                    if s:
                        filled(pe, s // STEPS)
                    else:
                        pe.wait_ge(s_half, 112)
                    first_step(s // STEPS)
                    continue
                if s == TB // 2:
                    filled(pe, 0)
                if 0 <= s < NSTEP:
                    scores(s)
                for job in jobs_at(s):
                    run(job)
                if 0 < s <= NSTEP:
                    values(s - 1)

        @block.vector
        def _(dve):
            links = [0]

            def link(ins):
                links[0] += 1
                ins.then_inc(s_chain, 1)
                dve.wait_ge(s_chain, links[0])

            counts = {}

            def tell(ins, s):
                counts[s.name] = counts.get(s.name, 0) + 1
                ins.then_inc(s, 1)
                dve.wait_ge(s, counts[s.name])

            link(dve.memset(ones_col[:], 1.0))
            link(dve.memset(opsum[:], 0.0))
            dve.wait_ge(s_bias, 16)
            link(dve.tensor_scalar(ang[:, 1, :], ang[:, 0, :], -2 * PI, 0.0, ALU.max, ALU.min))
            link(dve.tensor_scalar(ang[:, 1, :], ang[:, 1, :], PI, None, ALU.add))
            link(dve.scalar_tensor_tensor(ang[:, 2, :], ang[:, 1, :], -1.0, ang[:, 1, :], ALU.mult, ALU.min))
            tell(dve.tensor_scalar(ang[:, 2, :], ang[:, 2, :], PI / 2, None, ALU.add), s_angle)

            def key_angles(ct):
                if ct == 0:
                    dve.wait_ge(s_sin, 1)
                    link(dve.tensor_scalar(ang[:, 5, :], ang[:, 3, :], -1.0, None, ALU.mult))
                    link(dve.tensor_scalar(ang[:, 4, :], ang[:, 4, :], -1.0, None, ALU.mult))
                cosb, sinb, nsinb = ang[:, 4, ct:ct + 1], ang[:, 5, ct:ct + 1], ang[:, 3, ct:ct + 1]
                link(dve.tensor_scalar(ktrig[:, ct, 0, :], qtrig[:, 1, :], nsinb, None, ALU.mult))
                link(dve.scalar_tensor_tensor(ktrig[:, ct, 0, :], qtrig[:, 0, :], cosb,
                                              ktrig[:, ct, 0, :], ALU.mult, ALU.add))
                link(dve.tensor_scalar(ktrig[:, ct, 1, :], qtrig[:, 0, :], sinb, None, ALU.mult))
                link(dve.scalar_tensor_tensor(ktrig[:, ct, 1, :], qtrig[:, 1, :], cosb,
                                              ktrig[:, ct, 1, :], ALU.mult, ALU.add))

            def set_up():
                for i in range(2):
                    link(dve.memset(val[i][:, :, :, HD:HD + 1], 1.0))
                link(dve.memset(ones[:], 1.0))
                link(dve.memset(before[:], 0.0))
                dve.wait_ge(s_const, 16 * NCONST)
                link(dve.tensor_copy(tri[:], tri_f[:]))
                tell(dve.tensor_copy(blocks[:], blocks_f[:]), s_setup)

            def split_unit(c, i):
                ct, qk, half = c % KC, i % 2, i // 2
                u = 4 * c + i
                dve.wait_ge(s_soft, u + 1)
                if u == 0:
                    dve.wait_ge(s_trig, 16)
                tell(dve.scalar_tensor_tensor(raw[:], raw[:], 0.0, soft[:], ALU.max, ALU.add), s_raw)
                table = qtrig if qk == 0 else ktrig[:, ct]
                if u:
                    dve.wait_ge(s_split, u)
                link(dve.tensor_tensor(emb[:], raw[:].unsqueeze(1).to_broadcast((P, 2, HALF)),
                                       table[:, :, HALF * half:HALF * (half + 1)], ALU.mult))
                if u >= 2:
                    v = u - 2
                    stored(dve, v // 4, v % 4)
                tell(dve.tensor_copy(split[u % 2][:, 0], emb[:]), s_hi)

            def read_out(job):
                kind, c, i = (*job, 0)[:3]
                misc = bank(job)
                dve.wait_ge(s_full, number[job] + 1)
                if kind == "qk":
                    if u := 4 * c + i:
                        dve.wait_ge(s_square, u)
                    tell(dve.tensor_copy(raw[:], misc[:]), s_free)
                    tell(dve.scalar_tensor_tensor(soft[:], raw[:], -1.0, raw[:], ALU.mult, ALU.min), s_abs)
                elif kind == "v":
                    tell(dve.tensor_copy(val[c % 2][:, 2 * i:2 * i + 2, :, 0:HD],
                                         misc[:].rearrange("p (t h d) -> p t h d", t=2, h=HEADS)), s_free)
                elif kind == "norms":
                    qk, half = i % 2, i // 2
                    tell(dve.tensor_reduce(tops[:, 2 * qk + half:2 * qk + half + 1], misc[:], AX.X,
                                           ALU.max), s_free)
                    if i == 3:
                        for m in range(2):
                            link(dve.tensor_tensor(top2[:, m:m + 1], tops[:, 2 * m:2 * m + 1],
                                                   tops[:, 2 * m + 1:2 * m + 2], ALU.max))
                        link(dve.tensor_tensor(top2[:, 2:3], top2[:, 0:1], top2[:, 1:2], ALU.mult))
                        tell(dve.tensor_scalar(over[:], top2[:, 2:3], BOUND ** 2 * HD, None, ALU.is_gt),
                             s_over)
                elif kind == "count":
                    tell(dve.tensor_copy(flags[0:1, c:c + 1], misc[0:1, 0:1]), s_free)
                    tell(dve.memset(top2[:, 0:1], 0.0), s_flag)
                elif kind == "project":
                    b, t0, t1 = UNITS[c]
                    if i == 0:
                        dve.wait_ge(s_res, 16 * (b + 1))
                    r = res[:, 2 * i:2 * i + 2, 0:DIM]
                    tell(dve.tensor_tensor(r, misc[:].rearrange("p (t d) -> p t d", t=2), r, ALU.add),
                         s_free)
                    for t in (2 * i, 2 * i + 1):
                        link(dve.bn_stats(stats[:, t, :], res[:, t, 0:DIM]))
                        link(dve.bn_aggr(mv[:, t, :], stats[:, t, :]))
                    if 2 * i + 2 == t1:
                        tell(dve.tensor_scalar(lnt[:, 0, t0:t1], mv[:, t0:t1, 1], EPS, None, ALU.add),
                             s_var)
                elif kind == "turn":
                    tell(dve.tensor_copy(x1T[i % 2][:].rearrange("p t k n -> p (t k n)"), misc[:]), s_free)
                elif kind == "router":
                    tell(dve.tensor_tensor(
                        rt[:, 0, 2 * i:2 * i + 2, :],
                        misc[:, 0:2 * EXPERTS].rearrange("p (t e) -> p t e", e=EXPERTS),
                        br[:].unsqueeze(1).to_broadcast((P, 2, EXPERTS)), ALU.add), s_free)
                    b, t0, t1 = UNITS[c]
                    if 2 * i + 2 == t1:
                        link(dve.tensor_reduce(rs[:, 0, t0:t1], rt[:, 0, t0:t1], AX.X, ALU.max))
                        tell(dve.tensor_tensor(rt[:, 1, t0:t1], rt[:, 0, t0:t1],
                                               wide(rs[:, 0, t0:t1], t1 - t0), ALU.subtract), s_logit)
                elif kind == "place":
                    _, t0, t1 = UNITS[c]
                    tell(dve.tensor_copy(rt[:, 6, t0:t1].rearrange("p t e -> p (t e)"),
                                         misc[:, 0:(t1 - t0) * EXPERTS]), s_free)
                    slots(c)

            def wide(a, n):
                return a.unsqueeze(2).to_broadcast((P, n, EXPERTS))

            def norm(u, part):
                _, t0, t1 = UNITS[u]
                half = (t1 - t0) // 2
                if part == 0:
                    link(dve.tensor_copy(res[:, t0:t1, TOKEN],
                                         token_no[:, TB * UNITS[u][0] + t0:TB * UNITS[u][0] + t1]))
                    dve.wait_ge(s_rstd, u + 1)
                    newton(dve, link, lnt[:, :, t0:t1])
                for t in range(t0 + part * half, t0 + (part + 1) * half):
                    ins = dve.tensor_scalar(res[:, t, 0:DIM], res[:, t, 0:DIM], mv[:, t, 0:1],
                                            lnt[:, 4, t:t + 1], ALU.subtract, ALU.mult)
                    if t < t1 - 1:
                        link(ins)
                if part == 1:
                    tell(ins, s_x1)

            def top_two(u):
                b, t0, t1 = UNITS[u]
                T, n = slice(t0, t1), t1 - t0
                dve.wait_ge(s_gexp, u + 1)
                link(dve.tensor_reduce(rs[:, 1, T], rt[:, 1, T], AX.X, ALU.add))
                link(dve.reciprocal(rs[:, 2, T], rs[:, 1, T]))
                gates = res[:, T, GATES:GATES + EXPERTS]
                link(dve.tensor_tensor(gates, rt[:, 1, T], wide(rs[:, 2, T], n), ALU.mult))
                for k in range(2):
                    g, pick = (gates, rt[:, 3, T])[k], rt[:, 4 + k, T]
                    link(dve.tensor_reduce(rs[:, 3 + k, T], g, AX.X, ALU.max))
                    link(dve.tensor_tensor(rt[:, 7, T], g, wide(rs[:, 3 + k, T], n), ALU.is_equal))
                    link(dve.tensor_tensor(rt[:, 7, T], rt[:, 7, T], rev[:, T], ALU.mult))
                    link(dve.tensor_reduce(rs[:, 5, T], rt[:, 7, T], AX.X, ALU.max))
                    link(dve.tensor_tensor(pick, rt[:, 7, T], wide(rs[:, 5, T], n), ALU.is_equal))
                    if k == 0:
                        link(dve.scalar_tensor_tensor(rt[:, 3, T], pick, -4.0, g, ALU.mult, ALU.add))
                tell(dve.tensor_tensor(mask[:, T], rt[:, 4, T], rt[:, 5, T], ALU.add), s_mask)

            def slots(u):
                b, t0, t1 = UNITS[u]
                T = slice(t0, t1)
                with nc.allow_low_precision(reason="counts of tiles, below 256: exact"):
                    link(dve.tensor_reduce(rs[:, 6, 0:EXPERTS], mask[:, T].rearrange("p t e -> p e t"),
                                           AX.X, ALU.add))
                    link(dve.tensor_tensor(before[:], before[:], rs[:, 6, 0:EXPERTS], ALU.add))
                link(dve.tensor_scalar(rt[:, 8, T], rt[:, 6, T], float(CAP), float(OOB),
                                       ALU.is_gt, ALU.mult))
                link(dve.tensor_tensor(rt[:, 9, T], rt[:, 6, T], slot_base[:, T], ALU.add))
                link(dve.tensor_tensor(rt[:, 9, T], rt[:, 9, T], rt[:, 8, T], ALU.add))
                for k in range(2):
                    link(dve.tensor_tensor(rt[:, 10 + k, T], rt[:, 4 + k, T], rt[:, 9, T], ALU.mult))
                if t0 == 0 and b:
                    dve.wait_ge(s_scat, 16 * 2 * TB * b)
                with nc.allow_low_precision(reason="whole numbers below 2 ** 24: exact"):
                    for k in range(2):
                        ins = dve.tensor_reduce(scatter_idx[:, k, T], rt[:, 10 + k, T], AX.X, ALU.add)
                        if k == 0:
                            link(ins)
                tell(ins, s_idx)

            def read_outputs(blk):
                dve.wait_ge(s_pv, TB * (blk + 1))
                if blk:
                    dve.wait_ge(s_norm, blk)
                tell(dve.tensor_copy(oraw[:], opsum[:]), s_ofree)

            def sums(part):
                if part == 0:
                    link(dve.stream_shuffle(oden[:], oraw[:], [HD] * 32))
                half = oden[:, HALF // 2 * part:HALF // 2 * (part + 1)]
                tell(dve.reciprocal(half, half), s_sums)

            def general_maxima(grp):
                dve.wait_ge(s_flag, grp // 2 + 1)
                flag = dve.value_load(flags[0:1, grp // 2:grp // 2 + 1], min_val=0, max_val=P)
                with dve.If(flag > 0):
                    full, free = (GEN + 1) * grp, (GEN + 2) * grp
                    for m in range(GEN):
                        dve.wait_ge(g_full, full + m + 1)
                        dve.tensor_reduce(gmax[:, m:m + 1], misc[:], AX.X, ALU.max).then_inc(g_free, 1)
                    dve.wait_ge(g_free, free + GEN)
                    dve.tensor_reduce(gneg[:], gmax[:].rearrange("p (m h) -> p m h", h=2), AX.X, ALU.max,
                                      negate=True).then_inc(g_free, 1)
                    dve.wait_ge(g_full, full + GEN + 1)
                    dve.tensor_copy(grow[:], misc[0:GH * TB, 0:P]).then_inc(g_free, 1)
                    dve.wait_ge(g_free, free + GEN + 2)
                with dve.Else():
                    dve.sem_inc(g_free, GEN + 2)

            for s in range(first, last + 1):
                if 0 < s <= NSTEP and s % TB == 0:
                    read_outputs(s // TB - 1)
                if 0 <= s < NSTEP and s % STEPS == 0:
                    general_maxima(s // STEPS)
                for job in jobs_at(s):
                    read_out(job)
                for job in jobs_at(s - 2):
                    if job[0] == "qk":
                        split_unit(*job[1:])
                if s == first + 3:
                    set_up()
                    key_angles(0)
                if s == -1:
                    key_angles(1)
                for part in range(2):
                    if sums_at(s, part) is not None:
                        sums(part)
                if (u := tail_at(s, "norm")) is not None:
                    norm(u, 0)
                if (u := tail_at(s, "norm2")) is not None:
                    norm(u, 1)
                if (u := tail_at(s, "top")) is not None:
                    top_two(u)


def newton(dve, link, lnt):
    link(dve.tensor_tensor(lnt[:, 3, :], lnt[:, 2, :], lnt[:, 2, :], ALU.mult))
    link(dve.tensor_tensor(lnt[:, 3, :], lnt[:, 3, :], lnt[:, 0, :], ALU.mult))
    link(dve.tensor_scalar(lnt[:, 3, :], lnt[:, 3, :], -0.5, 1.5, ALU.mult, ALU.add))
    link(dve.tensor_tensor(lnt[:, 4, :], lnt[:, 2, :], lnt[:, 3, :], ALU.mult))


def experts(nc, w1_d, b1_d, w2_d, b2_d, tile_d, disp_d, sum_d, ident, areas, out):
    TERMS = ((0, 0), (0, 1), (1, 0))
    with ExitStack() as ctx:
        sb = lambda name, shape, dt=F32: ctx.enter_context(nc.sbuf_tensor(name, shape, dt))
        sem = lambda name: ctx.enter_context(nc.semaphore(name))
        raw1, raw2, w1s_0, w2s_0 = weight_views(areas)
        w1s = [w1s_0, sb("w1s", [P, 2, KC, HIDDEN], F32R)[:]]
        w2s = [w2s_0, sb("w2s", [P, 2, HK, DIM], F32R)[:]]
        b1 = sb("b1", [P, EXPERTS, HK])
        b2 = sb("b2", [P, EXPERTS, DIM])
        tile_no = sb("tile_no", [P, ST])
        both_rows = sb("rows", [P, 2 * ST * WIDE])
        rows = [both_rows[:, ST * WIDE * i:ST * WIDE * (i + 1)].rearrange("p (t d) -> p t d", t=ST)
                for i in range(2)]
        gate = [sb(f"gate{i}", [P, ST]) for i in range(2)]
        extra = sb("extra", [P, ST])
        add_idx = [sb(f"add_idx{i}", [P, ST], I32) for i in range(2)]
        xe = [sb(f"xe{i}", [P, 2, KC, CAP], F32R) for i in range(2)]
        NH = 3
        hraw = [sb(f"hraw{i}", [P, CAP]) for i in range(NH)]
        hid = sb("hid", [P, 2 * HK * CAP], F32R)
        hids = hid[:].rearrange("p (s k n) -> p s k n", s=2, k=HK)
        biased = [sb(f"biased{i}", [P, DIM]) for i in range(2)]
        eo = [sb(f"eo{i}", [P, ST, DIM]) for i in range(2)]
        area_k = areas[0]
        half = KC * SEQ
        y = [area_k[:, half * i:half * (i + 1)].rearrange("p (t d) -> p t d", t=TB) for i in range(2)]
        y += [b2[:].rearrange("p e d -> p (e d)")[:, 0:TB * DIM].rearrange("p (t d) -> p t d", t=TB),
              both_rows[:, 0:TB * DIM].rearrange("p (t d) -> p t d", t=TB)]
        stats = [sb(f"stats2_{i}", [P, TB, 6]) for i in range(2)]
        mv = sb("mv2", [P, BATCH, TB, 2])
        lnt = [sb(f"lnt2_{b}", [P, 6, TB]) for b in range(BATCH)]
        CHUNKS = [(0, 0, TB // 2), (0, TB // 2, TB)]
        CHUNKS += [(b, 0, TB) for b in range(1, BATCH - 1)]
        CHUNKS += [(BATCH - 1, 0, TB // 2), (BATCH - 1, TB // 2, TB)]

        def share(n, eighths):
            _, t0, t1 = CHUNKS[n]
            return range(*(t0 + (t1 - t0) * i // 8 for i in eighths))

        POOL_SHARE, ACT_SHARE = (0, 3), (3, 8)
        hp = [ctx.enter_context(nc.psum_tensor(f"hp{i}", [P, 2, HALF], F32)) for i in range(2)]
        yp = [ctx.enter_context(nc.psum_tensor(f"yp{i}", [P, HALF], F32)) for i in range(2)]
        tp = [ctx.enter_context(nc.psum_tensor(f"tp{i}", [P, HALF], F32)) for i in range(2)]

        s_b1, s_bias, s_w = sem("s_b1"), sem("s_bias2"), sem("s_w")
        s_whi, s_wlo = sem("s_whi2"), sem("s_wlo2")
        s_rows = [sem(f"s_rows{i}") for i in range(2)]
        s_turn, s_xhi, s_turned = sem("s_turn"), sem("s_xhi"), sem("s_turned")
        s_h, s_gelu, s_hhi, s_hid = sem("s_h"), sem("s_gelu"), sem("s_hhi"), sem("s_hid")
        s_y, s_biased, s_eo, s_add = sem("s_y"), sem("s_biased"), sem("s_eo"), sem("s_add")
        s_index = sem("s_index")
        s_donep = sem("s_done_pool")
        s_load = [sem(f"s_load{n}") for n in range(len(CHUNKS))]
        s_var, s_rstd = sem("s_var2"), sem("s_rstd2")
        s_shift, s_donea, s_out = sem("s_shift"), sem("s_done_act"), sem("s_out")
        s_chain, s_actchain = sem("s_chain2"), sem("s_actchain2")
        block = ctx.enter_context(nc.Block())

        TURNS = ((0,), (1,), (2,), (3,), (4,))

        @block.sync
        def _(sp):
            def load_rows(e):
                if e >= 2:
                    sp.wait_ge(s_index, e - 1)
                sp.dma_start(rows[e % 2], disp_d[e * CAP:(e + 1) * CAP].rearrange("(t p) d -> p t d", p=P)
                             ).then_inc(s_rows[e % 2], 16)

            def load_weights(e):
                if e >= 2:
                    sp.wait_ge(s_wlo, 2 * (e - 1))
                sp.dma_start(raw1, w1_d[e].rearrange("(k p) n -> p k n", p=P)).then_inc(s_w, 16)
                sp.dma_start(raw2, w2_d[e].rearrange("(k p) n -> p k n", p=P)).then_inc(s_w, 16)

            load_rows(0)
            sp.dma_start(b1[:], b1_d).then_inc(s_b1, 16)
            sp.dma_start(tile_no[:], tile_d).then_inc(s_bias, 16)
            load_rows(1)
            load_weights(1)
            sp.dma_start(b2[:].rearrange("p e d -> p (e d)"), b2_d.to_broadcast((P, EXPERTS * DIM))
                         ).then_inc(s_bias, 16)
            for e in range(2, EXPERTS):
                load_rows(e)
                load_weights(e)
            sp.wait_ge(s_add, 16 * ST * EXPERTS)
            for n, (b, t0, t1) in enumerate(CHUNKS):
                sp.dma_start(y[b][:, t0:t1, :],
                             sum_d[b * SEQ + P * t0:b * SEQ + P * t1].rearrange("(t p) d -> p t d", p=P)
                             ).then_inc(s_load[n], 16)
            for n, (b, t0, t1) in enumerate(CHUNKS):
                sp.wait_ge(s_donea, n + 1)
                sp.wait_ge(s_donep, n + 1)
                sp.dma_start(out[b, P * t0:P * t1].rearrange("(t p) d -> p t d", p=P),
                             y[b][:, t0:t1, :]).then_inc(s_out, 16)
            sp.wait_ge(s_out, 16 * len(CHUNKS))

        @block.gpsimd
        def _(pool):
            def weight_remainders(e):
                for n, (raw_w, parts_w) in enumerate(((raw1, w1s[e % 2]), (raw2, w2s[e % 2]))):
                    pool.wait_ge(s_whi, 2 * (e - 1) + n + 1)
                    pool.tensor_tensor(parts_w[:, 1], raw_w, parts_w[:, 0].bitcast(F32),
                                       ALU.subtract).then_inc(s_wlo, 1)

            for e in range(EXPERTS):
                if e + 1 < EXPERTS:
                    weight_remainders(e + 1)
                pool.wait_ge(s_index, e + 1)
                if e:
                    pool.wait_ge(s_add, 16 * ST * e)
                for t in range(ST):
                    pool.wait_ge(s_eo, ST * e + t + 1)
                    pool.indirect_dma_start(
                        sum_d, bass.IndirectOffsetOnAxis(ap=add_idx[e % 2][:, t:t + 1], axis=0),
                        eo[e % 2][:, t, :], None, bounds_check=TOKENS + CAP - 1,
                        compute_op=ALU.add).then_inc(s_add, 16)
            for n, (b, _, _) in enumerate(CHUNKS):
                pool.wait_ge(s_shift, n + 1)
                for t in share(n, POOL_SHARE):
                    ins = pool.tensor_scalar(y[b][:, t, :], y[b][:, t, :], lnt[b][:, 4, t:t + 1],
                                             lnt[b][:, 5, t:t + 1], ALU.mult, ALU.add)
                ins.then_inc(s_donep, 1)

        @block.tensor
        def _(pe):
            def turn(e, t):
                n = ST * e + t
                pe.wait_ge(s_rows[e % 2], 16 * (e // 2 + 1))
                if n >= 2:
                    pe.wait_ge(s_turned, n - 1)
                for k in range(KC):
                    ins = pe.transpose(tp[n % 2][:, P * k:P * (k + 1)],
                                       rows[e % 2][:, t, P * k:P * (k + 1)], ident[:])
                ins.then_inc(s_turn, 1)

            for t in range(ST):
                turn(0, t)
            for e in range(EXPERTS):
                if e:
                    pe.wait_ge(s_wlo, 2 * e)
                for m in range(HK):
                    n = HK * e + m
                    if n >= 2:
                        pe.wait_ge(s_gelu, n - 1)
                    for h in range(2):
                        if m == 0:
                            pe.wait_ge(s_turned, ST * e + -(-CH * (h + 1) // P))
                        for k in range(KC):
                            for i, (a, b) in enumerate(TERMS):
                                ins = pe.matmul(hp[n % 2][:, h, 0:CH],
                                                w1s[e % 2][:, b, k, P * m:P * (m + 1)],
                                                xe[e % 2][:, a, k, CH * h:CH * (h + 1)],
                                                start=k == 0 and i == 0, stop=k == KC - 1 and i == 2)
                    ins.then_inc(s_h, 1)
                for t in range(ST):
                    if e + 1 < EXPERTS:
                        for tt in TURNS[t]:
                            turn(e + 1, tt)
                    n = ST * e + t
                    if n >= 2:
                        pe.wait_ge(s_biased, n - 1)
                    for m in range(HK):
                        if t == 0:
                            pe.wait_ge(s_hid, HK * e + m + 1)
                        for i, (a, b) in enumerate(TERMS):
                            ins = pe.matmul(yp[n % 2][:, 0:DIM], hids[:, a, m, P * t:P * (t + 1)],
                                            w2s[e % 2][:, b, m, :], start=m == 0 and i == 0,
                                            stop=m == HK - 1 and i == 2)
                    ins.then_inc(s_y, 1)

        @block.scalar
        def _(act):
            def weight_half(e, n):
                raw_w, parts_w = ((raw1, w1s[e % 2]), (raw2, w2s[e % 2]))[n]
                act.wait_ge(s_w, 32 * e)
                if e >= 2:
                    act.wait_ge(s_y, ST * (e - 1))
                act.copy(parts_w[:, 0], raw_w).then_inc(s_whi, 1)

            act.preload_act_table(ACT.Gelu)
            act.wait_ge(s_b1, 16)
            for e in range(EXPERTS):
                for m in range(HK):
                    n = HK * e + m
                    act.wait_ge(s_h, n + 1)
                    if n >= NH:
                        act.wait_ge(s_hid, n - NH + 1)
                    act.activation(hraw[n % NH][:].rearrange("p (h n) -> p h n", h=2), hp[n % 2][:, :, 0:CH],
                                   ACT.Gelu, bias=b1[:, e, m:m + 1]).then_inc(s_gelu, 1)
                    if e + 1 < EXPERTS and m in (2, 4):
                        weight_half(e + 1, m // 2 - 1)
                for t in range(ST):
                    act.wait_ge(s_biased, ST * e + t + 1)
                    if t == 0 and e >= 2:
                        act.wait_ge(s_add, 16 * ST * (e - 1))
                    act.mul(eo[e % 2][:, t, :], biased[(ST * e + t) % 2][:],
                            gate[e % 2][:, t:t + 1]).then_inc(s_eo, 1)
            act.preload_act_table_set("natural_log_exp_and_others")

            def rstd_guess(n):
                b, t0, t1 = CHUNKS[n]
                act.wait_ge(s_var, n + 1)
                act.activation(lnt[b][:, 1, t0:t1], lnt[b][:, 0, t0:t1], ACT.Ln).then_inc(s_actchain, 1)
                act.wait_ge(s_actchain, n + 1)
                act.activation(lnt[b][:, 2, t0:t1], lnt[b][:, 1, t0:t1], ACT.Exp,
                               scale=-0.5).then_inc(s_rstd, 1)

            def normalise(n):
                b = CHUNKS[n][0]
                act.wait_ge(s_shift, n + 1)
                for t in share(n, ACT_SHARE):
                    ins = act.activation(y[b][:, t, :], y[b][:, t, :], ACT.Identity,
                                         bias=lnt[b][:, 5, t:t + 1], scale=lnt[b][:, 4, t:t + 1])
                ins.then_inc(s_donea, 1)

            for n in range(len(CHUNKS) + 1):
                if n < len(CHUNKS):
                    rstd_guess(n)
                if n:
                    normalise(n - 1)

        @block.vector
        def _(dve):
            links = [0]

            def link(ins):
                links[0] += 1
                ins.then_inc(s_chain, 1)
                dve.wait_ge(s_chain, links[0])

            def turned(e, t):
                n = ST * e + t
                if t == 0 and e >= 2:
                    dve.wait_ge(s_h, HK * (e - 1))
                dve.wait_ge(s_turn, n + 1)
                src = tp[n % 2][:, 0:DIM].rearrange("p (k n) -> p k n", k=KC)
                hi, lo = (xe[e % 2][:, i, :, P * t:P * (t + 1)] for i in range(2))
                dve.tensor_copy(hi, src).then_inc(s_xhi, 1)
                dve.wait_ge(s_xhi, n + 1)
                dve.tensor_tensor(lo, src, hi.bitcast(F32), ALU.subtract).then_inc(s_turned, 1)

            def index(e):
                dve.wait_ge(s_rows[e % 2], 16 * (e // 2 + 1))
                token = rows[e % 2][:, :, TOKEN]
                if e >= 2:
                    dve.wait_ge(s_add, 16 * ST * (e - 1))
                link(dve.tensor_copy(gate[e % 2][:], rows[e % 2][:, :, GATES + e]))
                link(dve.scalar_tensor_tensor(extra[:], token, float(TOKENS), tile_no[:],
                                              ALU.is_ge, ALU.mult))
                dve.tensor_tensor(add_idx[e % 2][:], extra[:], token, ALU.add).then_inc(s_index, 1)
                dve.wait_ge(s_index, e + 1)

            for t in range(ST):
                turned(0, t)
            dve.wait_ge(s_bias, 32)
            for e in range(EXPERTS):
                for m in range(HK):
                    n = HK * e + m
                    dve.wait_ge(s_gelu, n + 1)
                    if m == 0 and e:
                        dve.wait_ge(s_y, ST * e)
                    dve.tensor_copy(hids[:, 0, m], hraw[n % NH][:]).then_inc(s_hhi, 1)
                    dve.wait_ge(s_hhi, n + 1)
                    dve.tensor_tensor(hids[:, 1, m], hraw[n % NH][:], hids[:, 0, m].bitcast(F32),
                                      ALU.subtract).then_inc(s_hid, 1)
                    if m == 1:
                        index(e)
                for t in range(ST):
                    if e + 1 < EXPERTS:
                        for tt in TURNS[t]:
                            turned(e + 1, tt)
                    n = ST * e + t
                    dve.wait_ge(s_y, n + 1)
                    if n >= 2:
                        dve.wait_ge(s_eo, n - 1)
                    dve.tensor_tensor(biased[n % 2][:], yp[n % 2][:, 0:DIM], b2[:, e, :], ALU.add
                                      ).then_inc(s_biased, 1)

            def variances(n):
                b, t0, t1 = CHUNKS[n]
                dve.wait_ge(s_load[n], 16)
                for t in range(t0, t1):
                    ins = dve.bn_stats(stats[n % 2][:, t, :], y[b][:, t, :])
                link(ins)
                for t in range(t0, t1):
                    ins = dve.bn_aggr(mv[:, b, t, :], stats[n % 2][:, t, :])
                link(ins)
                dve.tensor_scalar(lnt[b][:, 0, t0:t1], mv[:, b, t0:t1, 1], EPS, None, ALU.add
                                  ).then_inc(s_var, 1)
                dve.wait_ge(s_var, n + 1)

            def scale_and_shift(n):
                b, t0, t1 = CHUNKS[n]
                dve.wait_ge(s_rstd, n + 1)
                newton(dve, link, lnt[b][:, :, t0:t1])
                dve.scalar_tensor_tensor(lnt[b][:, 5, t0:t1], mv[:, b, t0:t1, 0], -1.0,
                                         lnt[b][:, 4, t0:t1], ALU.mult, ALU.mult).then_inc(s_shift, 1)

            for n in range(len(CHUNKS) + 1):
                if n < len(CHUNKS):
                    variances(n)
                if n:
                    scale_and_shift(n - 1)


def kernel(L0_attn_x, L0_attn_wq, L0_attn_wk, L0_attn_wv, L0_attn_wo, L0_attn_pope_bias,
           L0_ffn_router_w, L0_ffn_router_b, L0_ffn_w1, L0_ffn_b1, L0_ffn_w2, L0_ffn_b2):
    import numpy as np
    import concourse.bacc as bacc
    from concourse.bass_utils import run_bass_kernel_spmd

    def parts(a):
        a = np.asarray(a)
        return np.ascontiguousarray(a.reshape(-1, P, a.shape[1]).transpose(1, 0, 2))

    x = np.asarray(L0_attn_x)
    pos = np.arange(SEQ, dtype=np.float32)
    inv = (10000.0 ** -(np.arange(HD) / HD)).astype(np.float32)
    angle = (pos[None, :] * inv[:, None]).astype(np.float32).astype(np.float64)
    trig = np.stack([np.cos(angle), np.sin(angle)], axis=1).astype(np.float32)
    e = np.arange(EXPERTS, dtype=np.float32)
    arrays = {
        "x": np.ascontiguousarray(x.reshape(BATCH, TB, P, DIM).transpose(0, 2, 1, 3)),
        "xT": np.ascontiguousarray(x.reshape(BATCH, SEQ, KC, P).transpose(0, 3, 2, 1)),
        "wq": parts(np.asarray(L0_attn_wq).T),
        "wk": parts(np.asarray(L0_attn_wk).T),
        "wv": parts(np.asarray(L0_attn_wv).T),
        "wo": parts(np.asarray(L0_attn_wo).T),
        "bias": np.ascontiguousarray(np.asarray(L0_attn_pope_bias).reshape(KC, P).T),
        "wr": parts(L0_ffn_router_w),
        "br": np.asarray(L0_ffn_router_b).reshape(1, EXPERTS),
        "w1": np.ascontiguousarray(L0_ffn_w1),
        "b1": np.ascontiguousarray(np.asarray(L0_ffn_b1).reshape(EXPERTS, HK, P).transpose(2, 0, 1)),
        "w2": np.ascontiguousarray(L0_ffn_w2),
        "b2": np.ascontiguousarray(np.asarray(L0_ffn_b2).reshape(1, EXPERTS * DIM)),
        "trig": np.ascontiguousarray(np.tile(trig, (P // HD, 1, 1))),
        "ident": np.eye(P, dtype=np.float32),
        "tri": np.triu(np.ones((P, P), np.float32)),
        "blocks": np.kron(np.eye(P // HD, dtype=np.float32), np.ones((HD, HD), np.float32)),
        "rev": np.tile(EXPERTS - e, (P, TB)).astype(np.float32),
        "base": np.tile(e * CAP - 1, (P, TB)).astype(np.float32),
        "blank": np.pad(TOKENS + np.arange(P, dtype=np.float32)[:, None], ((0, 0), (TOKEN, 0))),
        "number": np.arange(TOKENS, dtype=np.float32).reshape(BATCH * TB, P).T.copy(),
        "tile": np.tile(P * np.arange(ST, dtype=np.float32), (P, 1)),
    }
    nc = bacc.Bacc("TRN2", target_bir_lowering=False, num_devices=1)
    args = [nc.dram_tensor(f"in_{n}", a.shape, mybir.dt.from_np(a.dtype), kind="ExternalInput").ap()
            for n, a in arrays.items()]
    out = nc.dram_tensor("out", (BATCH, SEQ, DIM), F32, kind="ExternalOutput").ap()
    build(nc, *args, out)
    r = run_bass_kernel_spmd(nc, [{f"in_{n}": a for n, a in arrays.items()}], core_ids=[0])
    return r.results[0]["out"]
```
